# Optimizing a Trainium2 kernel written in Bass

```python
import numpy as np
import jax
import jax.numpy as jnp

def _softmax(x, axis=-1):
    return jax.nn.softmax(x, axis=axis)
def _gelu(x):
    return jax.nn.gelu(x, approximate=True)
def _silu(x):
    return jax.nn.silu(x)
def _sigmoid(x):
    return jax.nn.sigmoid(x)
def _layernorm(x, axis=-1, eps=1e-5):
    m = jnp.mean(x, axis=axis, keepdims=True)
    v = jnp.var(x, axis=axis, keepdims=True)
    return (x - m) / jnp.sqrt(v + eps)
def _scatter_add(tgt, idx, src, axis=0):
    return tgt.at[idx].add(src)
def _segment_sum(src, seg, n):
    return jax.ops.segment_sum(src, seg, n)

kernel_name = 'mk_conv_preact_d2_conv_nhwc512_6874f9'

def setup_inputs(seed: int = 0):
    np.random.seed(seed)
    _w = jnp.asarray
    def _rec_inputs():
        import jax
        import jax.numpy as jnp
        _gk = jax.random.key(seed)
        x = -0.0002928 + 1 * jax.random.normal(jax.random.fold_in(_gk, 1), (8, 32, 32, 512), jnp.float32)
        return x
    x = _rec_inputs()
    def _L0_conv_setup():
        import jax, jax.numpy as jnp
        import numpy as np
        B, H, W, C = (8, 32, 32, 512)
        ATTN_DIM = 512
        NUM_HEADS = 8
        DIM_HEAD = ATTN_DIM // NUM_HEADS
        SCALE = DIM_HEAD ** (-0.5)
        GN_EPS = 0.001
        key = jax.random.key(seed)
        k1, k2, k3 = jax.random.split(key, 3)
        x = jax.random.normal(k1, (B, H, W, C), dtype=jnp.float32)
        w_qkv = jax.random.normal(k2, (C, 3 * ATTN_DIM), dtype=jnp.float32) * C ** (-0.5)
        w_out = jax.random.normal(k3, (ATTN_DIM, C), dtype=jnp.float32) * ATTN_DIM ** (-0.5)
        b_out = jnp.zeros((C,), dtype=jnp.float32)
        gamma = jnp.ones((C,), dtype=jnp.float32)
        beta = jnp.zeros((C,), dtype=jnp.float32)
        return {'x': x, 'w_qkv': w_qkv, 'w_out': w_out, 'b_out': b_out, 'gamma': gamma, 'beta': beta}
    _L0_conv_all = _L0_conv_setup()
    _L0_conv_in = {k: v for k, v in _L0_conv_all.items() if k in ('w_qkv', 'w_out', 'b_out', 'gamma', 'beta', )}
    del _L0_conv_all

    def _L1_conv_setup():
        import jax, jax.numpy as jnp
        import numpy as np
        from jax import lax
        C = 512
        B, T, N = (8, 16, 32)
        KSZ = 7
        NEG_SLOPE = 0.01
        LN_EPS = 1e-05
        key = jax.random.key(seed)
        ks = jax.random.split(key, 8)
        local_feat = jax.random.normal(ks[0], (B, T, N, C), dtype=jnp.float32)
        global_feat = jax.random.normal(ks[1], (B, C), dtype=jnp.float32)
        pos = jax.random.normal(ks[2], (B, T, N, 3), dtype=jnp.float32)
        W = jnp.eye(C, dtype=jnp.float32) + 0.01 * jax.random.normal(ks[3], (C, C), dtype=jnp.float32)
        conv_w = jax.random.normal(ks[4], (C, 1, KSZ), dtype=jnp.float32) * np.sqrt(2.0 / KSZ)
        conv_b = jnp.zeros((C,), dtype=jnp.float32)
        ln_gamma = jnp.ones((C,), dtype=jnp.float32)
        ln_beta = jnp.zeros((C,), dtype=jnp.float32)
        return {'local_feat': local_feat, 'global_feat': global_feat, 'pos': pos, 'W': W, 'conv_w': conv_w, 'conv_b': conv_b, 'ln_gamma': ln_gamma, 'ln_beta': ln_beta}
    _L1_conv_all = _L1_conv_setup()
    _L1_conv_in = {k: v for k, v in _L1_conv_all.items() if k in ('global_feat', 'pos', 'W', 'conv_w', 'conv_b', 'ln_gamma', 'ln_beta', )}
    del _L1_conv_all

    return {
        "x": x,
        "L0_conv_w_qkv": _L0_conv_in["w_qkv"],
        "L0_conv_w_out": _L0_conv_in["w_out"],
        "L0_conv_b_out": _L0_conv_in["b_out"],
        "L0_conv_gamma": _L0_conv_in["gamma"],
        "L0_conv_beta": _L0_conv_in["beta"],
        "L1_conv_global_feat": _L1_conv_in["global_feat"],
        "L1_conv_pos": _L1_conv_in["pos"],
        "L1_conv_W": _L1_conv_in["W"],
        "L1_conv_conv_w": _L1_conv_in["conv_w"],
        "L1_conv_conv_b": _L1_conv_in["conv_b"],
        "L1_conv_ln_gamma": _L1_conv_in["ln_gamma"],
        "L1_conv_ln_beta": _L1_conv_in["ln_beta"],
    }

def reference(x, L0_conv_w_qkv, L0_conv_w_out, L0_conv_b_out, L0_conv_gamma, L0_conv_beta, L1_conv_global_feat, L1_conv_pos, L1_conv_W, L1_conv_conv_w, L1_conv_conv_b, L1_conv_ln_gamma, L1_conv_ln_beta):
    import jax
    import jax.numpy as jnp
    def _L0_conv_ref(x, w_qkv, w_out, b_out, gamma, beta):
        import jax, jax.numpy as jnp
        import numpy as np
        B, H, W, C = (8, 32, 32, 512)
        ATTN_DIM = 512
        NUM_HEADS = 8
        DIM_HEAD = ATTN_DIM // NUM_HEADS
        SCALE = DIM_HEAD ** (-0.5)
        GN_EPS = 0.001
        b, h, w, c = x.shape
        n = h * w
        qkv = jnp.einsum('bhwc,cd->bhwd', x, w_qkv)
        q, k, v = jnp.split(qkv, 3, axis=-1)

        def to_heads(t):
            t = jnp.transpose(t, (0, 3, 1, 2))
            return t.reshape(b, NUM_HEADS, DIM_HEAD, n)
        q, k, v = (to_heads(q), to_heads(k), to_heads(v))
        sim = jnp.einsum('bndi,bndj->bnij', q * SCALE, k)
        attn = jax.nn.softmax(sim, axis=-1)
        out = jnp.einsum('bnij,bndj->bnid', attn, v)
        out = out.reshape(b, NUM_HEADS * DIM_HEAD, h, w)
        out = jnp.transpose(out, (0, 2, 3, 1))
        y = jnp.einsum('bhwa,am->bhwm', out, w_out) + b_out
        mean = jnp.mean(y, axis=(1, 2, 3), keepdims=True)
        var = jnp.var(y, axis=(1, 2, 3), keepdims=True)
        y = (y - mean) * jax.lax.rsqrt(var + GN_EPS)
        return y * gamma + beta

    def _L1_conv_ref(local_feat, global_feat, pos, W, conv_w, conv_b, ln_gamma, ln_beta):
        import jax, jax.numpy as jnp
        import numpy as np
        from jax import lax
        C = 512
        B, T, N = (8, 16, 32)
        KSZ = 7
        NEG_SLOPE = 0.01
        LN_EPS = 1e-05
        b, t, nd, c = local_feat.shape
        n = t * nd
        feat = local_feat.reshape(b, n, c)
        norm = feat / jnp.maximum(jnp.linalg.norm(feat, axis=-1, keepdims=True), 1e-12)
        A = jnp.einsum('bnc,cc,bcm->bnm', norm, W, jnp.swapaxes(norm, 1, 2))
        A = A.reshape(b, n, t, nd)
        top_A = jnp.argmax(A, axis=-1)
        top_feat = local_feat[jnp.arange(b)[:, None, None], jnp.arange(t)[None, None, :], top_A]
        x = jnp.swapaxes(top_feat.reshape(b * n, t, c), 1, 2)
        y = lax.conv_general_dilated(x, conv_w, window_strides=(1,), padding='VALID', dimension_numbers=('NCH', 'OIH', 'NCH'), feature_group_count=c)
        y = y + conv_b[None, :, None]
        y = jnp.swapaxes(y, 1, 2)
        mu = jnp.mean(y, axis=-1, keepdims=True)
        var = jnp.mean(jnp.square(y - mu), axis=-1, keepdims=True)
        ln = (y - mu) * lax.rsqrt(var + LN_EPS) * ln_gamma + ln_beta
        act = jnp.where(ln >= 0, ln, NEG_SLOPE * ln)
        out = jnp.mean(act, axis=1)
        return out.reshape(b, t, nd, c)

    def _gn(v, G=32, eps=1e-5):
        B_, H_, W_, C_ = v.shape
        g = v.reshape(B_, H_, W_, G, C_ // G)
        m = jnp.mean(g, axis=(1, 2, 4), keepdims=True)
        s = jnp.var(g, axis=(1, 2, 4), keepdims=True)
        return ((g - m) / jnp.sqrt(s + eps)).reshape(v.shape)

    def _ln_c(v, eps=1e-6):
        m = jnp.mean(v, axis=-1, keepdims=True)
        s = jnp.var(v, axis=-1, keepdims=True)
        return (v - m) / jnp.sqrt(s + eps)

    def _ln_t(v, eps=1e-5):
        m = jnp.mean(v, axis=-1, keepdims=True)
        s = jnp.var(v, axis=-1, keepdims=True)
        return (v - m) / jnp.sqrt(s + eps)

    def _to_tokens(v):
        B_, H_, W_, C_ = v.shape
        return v.reshape(B_, H_ * W_, C_)
    def _from_tokens(t, like):
        return t.reshape(like.shape)

    x = x + _L0_conv_ref(_gn(x), L0_conv_w_qkv, L0_conv_w_out, L0_conv_b_out, L0_conv_gamma, L0_conv_beta)
    x = x + _L1_conv_ref(_gn(x), L1_conv_global_feat, L1_conv_pos, L1_conv_W, L1_conv_conv_w, L1_conv_conv_b, L1_conv_ln_gamma, L1_conv_ln_beta)
    return x


_drawn_inputs = setup_inputs


def setup_inputs(seed=0):
    import zlib

    import numpy as np

    out = dict(_drawn_inputs(seed))
    spreads = {'L0_conv_b_out': (0.0, 0.1),
     'L0_conv_gamma': (1.0, 0.2),
     'L0_conv_beta': (0.0, 0.1),
     'L1_conv_conv_b': (0.0, 0.303),
     'L1_conv_ln_gamma': (1.0, 0.2),
     'L1_conv_ln_beta': (0.0, 0.1)}
    factors = {}
    for name, (base, spread) in spreads.items():
        noise = np.random.default_rng([zlib.crc32(name.encode()), seed]).standard_normal(out[name].shape)
        drawn = base * np.exp(spread * noise) if base else spread * noise
        out[name] = jnp.asarray(drawn.astype(out[name].dtype))
    for name, factor in factors.items():
        out[name] = (out[name] * factor).astype(out[name].dtype)
    return out
```

```python
from contextlib import ExitStack

import concourse.bass as bass
from concourse import mybir

F32 = mybir.dt.float32
F32R = mybir.dt.float32r
BF16 = mybir.dt.bfloat16
ALU = mybir.AluOpType
ACT = mybir.ActivationFunctionType
AX = mybir.AxisListType

P = 128
B = 8
N = 1024
C = 512
NT = N // P
KC = C // P
HEADS = 8
D = C // HEADS
G = B * HEADS
HALF = 512
GROUP = 16
NG = C // GROUP
T = 32
M = 32
KS = 7
TO = T - KS + 1
GN_IN_EPS = 1e-5
GN_OUT_EPS = 1e-3
LN_EPS = 1e-5
SCALE = float(D) ** -0.5


class Chain:

    def __init__(self, engine, sem, start):
        self.engine, self.sem, self.start, self.n = engine, sem, start, 0

    def __call__(self, instruction):
        instruction.then_inc(self.sem, 1)
        self.n += 1
        self.engine.wait_ge(self.sem, self.start + self.n)


def project_phase(nc, x, w_qkv, qk_hi, qk_lo, v_split):
    QKT = 2 * C // P
    TILES = QKT * 2 + NT
    BANKS = 4
    SCHAIN = 5
    with ExitStack() as ctx:
        def sb(name, shape, dt):
            return ctx.enter_context(nc.sbuf_tensor("p1_" + name, shape, dt))

        def psum(name, shape, dt=F32):
            return ctx.enter_context(nc.psum_tensor("p1_" + name, shape, dt))

        def sem(name):
            return ctx.enter_context(nc.semaphore("p1_" + name))

        ident = sb("ident", [P, P], F32)
        gavg = sb("gavg", [P, P], F32)
        w_raw = sb("w_raw", [P, KC, 3 * C], F32)
        w_h = sb("w_h", [P, KC, 3 * C], F32R)
        w_l = sb("w_l", [P, KC, 3 * C], F32R)
        x_tok = sb("x_tok", [P, NT, C], F32)
        x_ch = sb("x_ch", [P, KC, N], F32)
        x_h = sb("x_h", [P, KC, N], F32R)
        x_l = sb("x_l", [P, KC, N], F32R)
        qk_out = sb("qk_out", [P, 2, 2, N], F32R)
        v_out = sb("v_out", [P, 2, HEADS, 2, D], F32R)
        bn = sb("bn", [P, KC, 2, 6], F32)
        mv = sb("mv", [P, KC, 2], F32)
        gm = sb("gm", [P, KC], F32)
        dev = sb("dev", [P, KC], F32)
        spread = sb("spread", [P, KC], F32)
        gvar = sb("gvar", [P, KC], F32)
        gstd = sb("gstd", [P, KC], F32)
        grstd = sb("grstd", [P, KC], F32)
        turned = psum("turned", [P, 2, HALF])
        stat = psum("stat", [P, HALF])
        prod = psum("prod", [P, BANKS, HALF])

        consts = sem("consts")
        w_loaded = sem("w_loaded")
        w_high = sem("w_high")
        w_low = sem("w_low")
        x_loaded = sem("x_loaded")
        turn_full = sem("turn_full")
        xch_ready = sem("xch_ready")
        mv_ready = sem("mv_ready")
        mean_ready = sem("mean_ready")
        dev_ready = sem("dev_ready")
        var_ready = sem("var_ready")
        std_in = sem("std_in")
        std_out = sem("std_out")
        normed = sem("normed")
        hi_x = sem("hi_x")
        lo_x = sem("lo_x")
        prod_full = sem("prod_full")
        hi_done = sem("hi_done")
        lo_done = sem("lo_done")
        dchain = sem("dchain")
        qk_stored = [sem("qk_stored0"), sem("qk_stored1")]
        v_stored = [sem("v_stored0"), sem("v_stored1")]
        block = ctx.enter_context(nc.Block())

        @block.sync
        def _(sp):
            sp.dma_start(x_tok[:], x[0:N, :].rearrange("(t p) c -> p t c", p=P)).then_inc(x_loaded, 16)
            sp.dma_start(w_raw[:], w_qkv.rearrange("(k p) c -> p k c", p=P)).then_inc(w_loaded, 16)
            for k in range(2):
                sp.sem_inc(qk_stored[k], 16)
                sp.sem_inc(v_stored[k], 16)

            def stores(b):
                for m in range(QKT):
                    sp.wait_ge(lo_done, BANKS + b * TILES + 2 * m + 2)
                    row = m // (QKT // 2) * B * C + b * C + m % (QKT // 2) * P
                    sp.dma_start(qk_hi[bass.ds(row, P), :], qk_out[:, m % 2, 0, :].bitcast(F32)).then_inc(qk_stored[m % 2], 16)
                    sp.dma_start(qk_lo[bass.ds(row, P), :], qk_out[:, m % 2, 1, :].bitcast(F32)).then_inc(qk_stored[m % 2], 16)
                for t in range(NT):
                    sp.wait_ge(lo_done, BANKS + b * TILES + 2 * QKT + t + 1)
                    sp.dma_start(v_split[bass.ds(b * HEADS, HEADS), :, t, :].rearrange("h p c -> p h c"),
                                 v_out[:, t % 2].rearrange("p h a d -> p h (a d)").bitcast(F32)).then_inc(v_stored[t % 2], 16)

            with sp.Fori(0, B - 1) as b:
                sp.wait_ge(turn_full, b * 2 * KC + 2 * KC)
                sp.dma_start(x_tok[:], x[bass.ds(b * N + N, N), :].rearrange("(t p) c -> p t c", p=P)
                             ).then_inc(x_loaded, 16)
                stores(b)
            stores(B - 1)
            for k in range(2):
                sp.wait_ge(qk_stored[k], 16 + B * QKT * 16)
                sp.wait_ge(v_stored[k], 16 + B * NT // 2 * 16)

        @block.gpsimd
        def _(pool):
            pool.memset(ident[:], 0.0).then_inc(consts, 1)
            pool.memset(gavg[:], 1.0 / GROUP).then_inc(consts, 1)
            pool.wait_ge(consts, 2)
            pool.affine_select(out=ident[:], in_=ident[:], compare_op=ALU.not_equal, fill=1.0, base=0,
                               pattern=[[-1, P]], channel_multiplier=1).then_inc(consts, 1)
            blocks = gavg[:].rearrange("p (g c) -> p g c", c=GROUP)
            pool.affine_select(out=blocks, in_=blocks, compare_op=ALU.is_ge, fill=0.0, base=0,
                               pattern=[[-GROUP, P // GROUP], [0, GROUP]], channel_multiplier=1).then_inc(consts, 1)
            pool.wait_ge(consts, 4)
            pool.affine_select(out=blocks, in_=blocks, compare_op=ALU.is_ge, fill=0.0, base=GROUP - 1,
                               pattern=[[GROUP, P // GROUP], [0, GROUP]], channel_multiplier=-1).then_inc(consts, 1)
            with pool.Fori(0, B) as b:
                for k in range(KC):
                    pool.wait_ge(hi_x, b * KC + k + 1)
                    pool.tensor_tensor(x_l[:, k, :], x_ch[:, k, :], x_h[:, k, :].bitcast(F32),
                                       ALU.subtract).then_inc(lo_x, 1)

        @block.scalar
        def _(act):
            act.sem_inc(xch_ready, 2)
            act.wait_ge(w_loaded, 16)
            for k in range(KC):
                act.activation(w_h[:, k, :], w_raw[:, k, :], ACT.Copy).then_inc(w_high, 1)
            with act.Fori(0, B) as b:
                for g in range(2 * KC):
                    act.wait_ge(turn_full, b * 2 * KC + g + 1)
                    act.activation(x_ch[:, g // 2, g % 2 * HALF:(g % 2 + 1) * HALF], turned[:, g % 2, :],
                                   ACT.Copy).then_inc(xch_ready, 1)
                act.wait_ge(std_in, b + 1)
                act.activation(gstd[:], gvar[:], ACT.Sqrt).then_inc(std_out, 1)
                for k in range(KC):
                    act.wait_ge(normed, b * KC + k + 1)
                    act.activation(x_h[:, k, :], x_ch[:, k, :], ACT.Copy).then_inc(hi_x, 1)
                for m in range(QKT):
                    for j in range(2):
                        if j == 0:
                            act.wait_ge(qk_stored[m % 2], 16 + b * QKT * 16 + m // 2 * 32)
                        act.wait_ge(prod_full, b * TILES + 2 * m + j + 1)
                        act.activation(qk_out[:, m % 2, 0, j * HALF:(j + 1) * HALF], prod[:, (2 * m + j) % BANKS, :],
                                       ACT.Copy, scale=SCALE if m < QKT // 2 else 1.0).then_inc(hi_done, 1)
                for t in range(NT):
                    q = 2 * QKT + t
                    act.wait_ge(v_stored[t % 2], 16 + b * NT // 2 * 16 + t // 2 * 16)
                    act.wait_ge(prod_full, b * TILES + q + 1)
                    act.activation(v_out[:, t % 2, :, 0, :],
                                   prod[:, q % BANKS, :].rearrange("p (h d) -> p h d", d=D),
                                   ACT.Copy).then_inc(hi_done, 1)

        @block.vector
        def _(dve):
            dve.sem_inc(lo_done, BANKS)
            for k in range(KC):
                dve.wait_ge(w_high, k + 1)
                dve.tensor_tensor(w_l[:, k, :], w_raw[:, k, :], w_h[:, k, :].bitcast(F32),
                                  ALU.subtract).then_inc(w_low, 1)
            with dve.Fori(0, B) as b:
                link = Chain(dve, dchain, b * SCHAIN)
                for g in range(2 * KC):
                    dve.wait_ge(xch_ready, 2 + b * 2 * KC + g + 1)
                    ins = dve.bn_stats(bn[:, g // 2, g % 2, :], x_ch[:, g // 2, g % 2 * HALF:(g % 2 + 1) * HALF])
                link(ins)
                dve.memset(dev[:], 0.0)
                for k in range(KC):
                    ins = dve.bn_aggr(mv[:, k, :], bn[:, k, :, :].rearrange("p a s -> p (a s)"))
                ins.then_inc(mv_ready, 1)
                dve.wait_ge(mean_ready, b + 1)
                link(dve.tensor_copy(gm[:], stat[:, 0:KC]))
                link(dve.tensor_tensor(dev[:], mv[:, :, 0], gm[:], ALU.subtract))
                link(dve.tensor_tensor(dev[:], dev[:], dev[:], ALU.mult))
                dve.tensor_tensor(spread[:], dev[:], mv[:, :, 1], ALU.add).then_inc(dev_ready, 1)
                dve.wait_ge(var_ready, b + 1)
                dve.tensor_scalar(gvar[:], stat[:, KC:2 * KC], GN_IN_EPS, None, ALU.add).then_inc(std_in, 1)
                dve.wait_ge(std_out, b + 1)
                link(dve.reciprocal(grstd[:], gstd[:]))
                for k in range(KC):
                    dve.tensor_scalar(x_ch[:, k, :], x_ch[:, k, :], gm[:, k:k + 1], grstd[:, k:k + 1],
                                      ALU.subtract, ALU.mult).then_inc(normed, 1)
                for m in range(QKT):
                    for j in range(2):
                        q = 2 * m + j
                        hi = qk_out[:, m % 2, 0, j * HALF:(j + 1) * HALF].bitcast(F32)
                        dve.wait_ge(hi_done, b * TILES + q + 1)
                        dve.scalar_tensor_tensor(qk_out[:, m % 2, 1, j * HALF:(j + 1) * HALF],
                                                 prod[:, q % BANKS, :], SCALE if m < QKT // 2 else 1.0, hi,
                                                 ALU.mult, ALU.subtract).then_inc(lo_done, 1)
                for t in range(NT):
                    q = 2 * QKT + t
                    dve.wait_ge(hi_done, b * TILES + q + 1)
                    dve.tensor_tensor(v_out[:, t % 2, :, 1, :],
                                      prod[:, q % BANKS, :].rearrange("p (h d) -> p h d", d=D),
                                      v_out[:, t % 2, :, 0, :].bitcast(F32), ALU.subtract).then_inc(lo_done, 1)
                assert link.n == SCHAIN

        @block.tensor
        def _(pe):
            pe.wait_ge(consts, 5)
            pe.wait_ge(w_low, KC)
            with pe.Fori(0, B) as b:
                pe.wait_ge(x_loaded, b * 16 + 16)
                for g in range(2 * KC):
                    pe.wait_ge(xch_ready, b * 2 * KC + g + 1)
                    for j in range(4):
                        t = g % 2 * 4 + j
                        ins = pe.transpose(turned[:, g % 2, j * P:(j + 1) * P],
                                           x_tok[:, t, g // 2 * P:(g // 2 + 1) * P], ident[:])
                    ins.then_inc(turn_full, 1)
                pe.wait_ge(mv_ready, b + 1)
                pe.matmul(stat[:, 0:KC], gavg[:], mv[:, :, 0], start=True, stop=True).then_inc(mean_ready, 1)
                pe.wait_ge(dev_ready, b + 1)
                pe.matmul(stat[:, KC:2 * KC], gavg[:], spread[:], start=True, stop=True).then_inc(var_ready, 1)
                pe.wait_ge(lo_x, b * KC + KC)
                parts = ((w_h, x_h), (w_h, x_l), (w_l, x_h))
                for q in range(TILES):
                    bank = prod[:, q % BANKS, :]
                    pe.wait_ge(lo_done, b * TILES + q + 1)
                    for n, (w, xx) in enumerate(parts):
                        for k in range(KC):
                            flags = dict(start=(n == 0 and k == 0), stop=(n == 2 and k == KC - 1))
                            if q < 2 * QKT:
                                m, j = q // 2, q % 2
                                ins = pe.matmul(bank, w[:, k, m * P:(m + 1) * P], xx[:, k, j * HALF:(j + 1) * HALF],
                                                **flags)
                            else:
                                t = q - 2 * QKT
                                ins = pe.matmul(bank, xx[:, k, t * P:(t + 1) * P], w[:, k, 2 * C:3 * C], **flags)
                    ins.then_inc(prod_full, 1)


def attention_phase(nc, qk_hi, qk_lo, v_split, attended):
    STEPS = NT
    QUARTERS = 4
    with ExitStack() as ctx:
        def sb(name, shape, dt):
            return ctx.enter_context(nc.sbuf_tensor("p2_" + name, shape, dt))

        def psum(name, shape, dt=F32):
            return ctx.enter_context(nc.psum_tensor("p2_" + name, shape, dt))

        def sem(name):
            return ctx.enter_context(nc.semaphore("p2_" + name))

        ident = sb("ident", [P, P], F32)
        twice = sb("twice", [P, D], F32)
        k_st = sb("k_st", [P, 2, N], F32R)
        q_hh = sb("q_hh", [P, 2, N], F32R)
        q_l0 = sb("q_l0", [P, 2, N], F32R)
        v_st = sb("v_st", [P, 2, NT, 2 * D], F32R)
        expd = sb("expd", [P, 2, N], F32)
        e_h = sb("e_h", [P, 2, NT, HALF], F32R)
        e_l = sb("e_l", [P, 2, NT, HALF], F32R)
        o_sb = sb("o_sb", [P, 2, HALF], F32)
        res = sb("res", [P, 2, 4, D], F32)
        nmax = sb("nmax", [P, STEPS], F32)
        rows = sb("rows", [P, 2, STEPS], F32)
        rinv = sb("rinv", [P, 2, 4], F32)
        score = psum("score", [P, 2, N])
        turned = psum("turned", [P, 2, HALF])
        out_ps = psum("out_ps", [P, HALF])
        row_ps = psum("row_ps", [P, HALF])

        consts = sem("consts")
        zeroed = sem("zeroed")
        kq_loaded = [sem("kq_loaded0"), sem("kq_loaded1")]
        v_loaded = [sem("v_loaded0"), sem("v_loaded1")]
        scored = sem("scored")
        maxed = sem("maxed")
        exped = sem("exped")
        turn_full = sem("turn_full")
        hi_done = sem("hi_done")
        lo_done = sem("lo_done")
        av_done = sem("av_done")
        o_copied = sem("o_copied")
        rows_full = sem("rows_full")
        rinv_done = sem("rinv_done")
        res_done = sem("res_done")
        stored = [sem("stored0"), sem("stored1")]
        def in_pairs(engine, pair):
            pair(0, True, False)
            with engine.Fori(2, G - 2, 2) as g:
                pair(g, False, False)
            pair(G - 2, False, True)

        block = ctx.enter_context(nc.Block())

        @block.gpsimd
        def _(pool):
            pool.memset(ident[:], 0.0).then_inc(consts, 1)
            pool.memset(twice[:], 0.0).then_inc(consts, 1)
            pool.wait_ge(consts, 2)
            pool.affine_select(out=ident[:], in_=ident[:], compare_op=ALU.not_equal, fill=1.0, base=0,
                               pattern=[[-1, P]], channel_multiplier=1).then_inc(consts, 1)
            pool.affine_select(out=twice[:], in_=twice[:], compare_op=ALU.not_equal, fill=1.0, base=0,
                               pattern=[[-1, D]], channel_multiplier=1).then_inc(consts, 1)
            pool.wait_ge(consts, 4)
            pool.affine_select(out=twice[:], in_=twice[:], compare_op=ALU.not_equal, fill=1.0, base=-D,
                               pattern=[[-1, D]], channel_multiplier=1).then_inc(consts, 1)

        @block.sync
        def _(sp):
            def load(g, k):
                q_row, k_row = g * D, B * C + g * D
                for at, row, dst, src in ((0, k_row, k_st, qk_hi), (D, k_row, k_st, qk_lo),
                                          (0, q_row, q_hh, qk_hi), (D, q_row, q_hh, qk_hi),
                                          (0, q_row, q_l0, qk_lo)):
                    sp.dma_start(dst[at:at + D, k, :].bitcast(F32), src[bass.ds(row, D), :]).then_inc(kq_loaded[k], 16)
                sp.dma_start(v_st[:, k].bitcast(F32), v_split[bass.ds(g, 1)].rearrange("o p t c -> p (o t) c")
                             ).then_inc(v_loaded[k], 16)

            def store(g, h, k):
                sp.wait_ge(res_done, 1 + 2 * g + h + 1)
                sp.dma_start(attended[bass.ds(g, 1), h * HALF:(h + 1) * HALF, :].rearrange("o (t p) d -> p (o t) d", p=P),
                             res[:, h]).then_inc(stored[h], 16)

            def pair(g, first=False, last=False):
                for k in range(2):
                    if not (last and k == 1):
                        if not (first and k == 0):
                            sp.wait_ge(av_done, 2 * (g + k))
                        load(g + k + 1, (k + 1) % 2)
                    if not (first and k == 0):
                        store(g + k - 1, 1, (k + 1) % 2)
                    store(g + k, 0, k)

            sp.sem_inc(stored[0], 16)
            sp.sem_inc(stored[1], 16)
            load(0, 0)
            in_pairs(sp, pair)
            store(G - 1, 1, 1)
            for h in range(2):
                sp.wait_ge(stored[h], 16 + 16 * G)

        @block.tensor
        def _(pe):
            def scores(g, k, s):
                n = g * STEPS + s
                if s == 0:
                    pe.wait_ge(kq_loaded[k], 80 * (g // 2 + 1) if isinstance(g, int) else (g + 2 - k) * 40)
                if not (isinstance(n, int) and n < 2):
                    pe.wait_ge(exped, n - 1)
                for j in range(2):
                    for part, q in enumerate((q_hh, q_l0)):
                        ins = pe.matmul(score[:, s % 2, j * HALF:(j + 1) * HALF], q[:, k, s * P:(s + 1) * P],
                                        k_st[:, k, j * HALF:(j + 1) * HALF], start=part == 0, stop=part == 1)
                ins.then_inc(scored, 1)

            def turn(g, k, s):
                n = g * STEPS + s
                pe.wait_ge(exped, n + 1)
                for j in range(2):
                    pe.wait_ge(lo_done, 2 * n + j + 1)
                    for i in range(4):
                        t = 4 * j + i
                        ins = pe.transpose(turned[:, j, i * P:(i + 1) * P], expd[:, s % 2, t * P:(t + 1) * P], ident[:])
                    ins.then_inc(turn_full, 1)

            def av(g, k, h, r):
                n = 2 * g + h
                if r == 0:
                    pe.wait_ge(lo_done, 2 + 8 * n + 8)
                    pe.wait_ge(o_copied, n + 1)
                    if h == 0:
                        pe.wait_ge(v_loaded[k], 16 * (g // 2 + 1) if isinstance(g, int) else (g + 2 - k) * 8)
                for t in (2 * r, 2 * r + 1):
                    for part, e in enumerate((e_h, e_l)):
                        ins = pe.matmul(out_ps[:], v_st[:, k, t, :], e[:, h, t, :],
                                        start=t == 0 and part == 0, stop=t == NT - 1 and part == 1)
                if r == QUARTERS - 1:
                    ins.then_inc(av_done, 1)

            def to_rows(g, h):
                n = 2 * g + h
                pe.wait_ge(o_copied, 1 + n + 1)
                pe.wait_ge(res_done, n + 1)
                for i in range(4):
                    ins = pe.matmul(row_ps[:, i * D:(i + 1) * D], o_sb[:, h, i * P:(i + 1) * P], twice[:],
                                    start=True, stop=True)
                ins.then_inc(rows_full, 1)

            def pair(g0, first, last):
                for k in range(2):
                    g = g0 + k
                    for s in range(STEPS):
                        if s < STEPS - 1:
                            scores(g, k, s + 1)
                        elif not (last and k == 1):
                            scores(g + 1, 1 - k, 0)
                        turn(g, k, s)
                        early = first and k == 0
                        if s < 4:
                            if not early:
                                av(g - 1, 1 - k, 1, s)
                        else:
                            av(g, k, 0, s - 4)
                        if s == 0 and not early:
                            to_rows(g - 1, 0)
                        if s == 4 and not early:
                            to_rows(g - 1, 1)

            pe.wait_ge(consts, 5)
            pe.wait_ge(zeroed, 1)
            scores(0, 0, 0)
            in_pairs(pe, pair)
            for r in range(QUARTERS):
                av(G - 1, 1, 1, r)
            to_rows(G - 1, 0)
            to_rows(G - 1, 1)

        @block.scalar
        def _(act):
            def exp(g, k, s):
                n = g * STEPS + s
                act.wait_ge(maxed, n + 1)
                if not (isinstance(n, int) and n < 2):
                    act.wait_ge(turn_full, 2 * (n - 1))
                act.activation(expd[:, s % 2, :], score[:, s % 2, :], ACT.Exp, bias=nmax[:, s:s + 1],
                               accum_out=rows[:, k, s:s + 1]).then_inc(exped, 1)

            def high(g, s):
                n = g * STEPS + s
                for j in range(2):
                    act.wait_ge(turn_full, 2 * n + j + 1)
                    if s % 4 == 0 and not (isinstance(g, int) and g == 0):
                        act.wait_ge(av_done, 2 * g - 2 + s // 4 + 1)
                    act.activation(e_h[:, s // 4, 4 * j:4 * j + 4, s % 4 * P:(s % 4 + 1) * P],
                                   turned[:, j, :].rearrange("p (t i) -> p t i", i=P), ACT.Copy).then_inc(hi_done, 1)

            def copy_out(g, h):
                n = 2 * g + h
                act.wait_ge(av_done, n + 1)
                act.activation(o_sb[:, h, :], out_ps[:], ACT.Copy).then_inc(o_copied, 1)

            def pair(g0, first, last):
                for k in range(2):
                    g = g0 + k
                    for s in range(STEPS):
                        if s == 0 and not (first and k == 0):
                            copy_out(g - 1, 0)
                        if s == 4 and not (first and k == 0):
                            copy_out(g - 1, 1)
                        high(g, s)
                        if s < STEPS - 1:
                            exp(g, k, s + 1)
                        elif not (last and k == 1):
                            exp(g + 1, 1 - k, 0)

            act.sem_inc(o_copied, 1)
            exp(0, 0, 0)
            in_pairs(act, pair)
            copy_out(G - 1, 0)
            copy_out(G - 1, 1)

        @block.vector
        def _(dve):
            def maximum(g, s):
                n = g * STEPS + s
                dve.wait_ge(scored, n + 1)
                dve.tensor_reduce(nmax[:, s:s + 1], score[:, s % 2, :], AX.X, ALU.max, negate=True).then_inc(maxed, 1)

            def low(g, s):
                n = g * STEPS + s
                for j in range(2):
                    dve.wait_ge(hi_done, 2 * n + j + 1)
                    part = [x[:, s // 4, 4 * j:4 * j + 4, s % 4 * P:(s % 4 + 1) * P] for x in (e_h, e_l)]
                    dve.tensor_tensor(part[1], turned[:, j, :].rearrange("p (t i) -> p t i", i=P),
                                      part[0].bitcast(F32), ALU.subtract).then_inc(lo_done, 1)

            def finish(g, k, h):
                n = 2 * g + h
                dve.wait_ge(rows_full, n + 1)
                dve.reciprocal(rinv[:, h, :], rows[:, k, 4 * h:4 * h + 4]).then_inc(rinv_done, 1)
                dve.wait_ge(rinv_done, n + 1)
                dve.wait_ge(stored[h], 16 + 16 * g)
                dve.tensor_tensor(res[:, h], row_ps[:, 0:4 * D].rearrange("p (t d) -> p t d", d=D),
                                  rinv[:, h, :].unsqueeze(2).to_broadcast([P, 4, D]), ALU.mult).then_inc(res_done, 1)

            def pair(g0, first, last):
                for k in range(2):
                    g = g0 + k
                    for s in range(STEPS):
                        if s < STEPS - 1:
                            maximum(g, s + 1)
                        elif not (last and k == 1):
                            maximum(g + 1, 0)
                        low(g, s)
                        if s == 0 and not (first and k == 0):
                            finish(g - 1, 1 - k, 0)
                        if s == 4 and not (first and k == 0):
                            finish(g - 1, 1 - k, 1)

            dve.memset(q_l0[D:P, :, :].bitcast(F32), 0.0).then_inc(zeroed, 1)
            dve.sem_inc(lo_done, 2)
            dve.sem_inc(res_done, 1)
            maximum(0, 0)
            in_pairs(dve, pair)
            finish(G - 1, 1, 0)
            finish(G - 1, 1, 1)


def mixing_phase(nc, x, attended, w_out, b_out, gamma, beta, w_diag, x_mid, feat_rows, chosen):
    BANKS = 4
    DCHAIN = 8
    with ExitStack() as ctx:
        def sb(name, shape, dt=F32):
            return ctx.enter_context(nc.sbuf_tensor("p3_" + name, shape, dt))

        def psum(name, shape, dt=F32):
            return ctx.enter_context(nc.psum_tensor("p3_" + name, shape, dt))

        def sem(name):
            return ctx.enter_context(nc.semaphore("p3_" + name))

        ident = sb("ident", [P, P])
        ident_b = sb("ident_b", [P, P], BF16)
        all_avg = sb("all_avg", [P, P])
        grp_avg = sb("grp_avg", [P, P])
        ramp = sb("ramp", [P, M], BF16)
        w_raw = sb("w_raw", [P, KC, C])
        w_h = sb("w_h", [P, KC, C], F32R)
        w_l = sb("w_l", [P, KC, C], F32R)
        bias = sb("bias", [P, C])
        gam = sb("gam", [P, C])
        bet = sb("bet", [P, C])
        gam_r = sb("gam_r", [P, C])
        diag = sb("diag", [P, KC])
        o_raw = sb("o_raw", [P, KC, N])
        x_tok = sb("x_tok", [P, NT, C])
        y = sb("y", [P, NT, C])
        work = sb("work", [P, NT, C])
        n_h = sb("n_h", [P, KC, N], F32R)
        n_l = sb("n_l", [P, KC, N], F32R)
        m_h = sb("m_h", [P, KC, N], F32R)
        m_l = sb("m_l", [P, KC, N], F32R)
        ysum = sb("ysum", [P, NT])
        ysq = sb("ysq", [P, NT])
        col = sb("col", [P, 8])
        gmean = sb("gmean", [P, NG])
        gvar = sb("gvar", [P, NG])
        gstd = sb("gstd", [P, NG])
        grstd = sb("grstd", [P, NG])
        nsq = sb("nsq", [P, NT])
        nstd = sb("nstd", [P, NT])
        nrec = sb("nrec", [P, NT])
        top = sb("top", [P, 2, T])
        equal = sb("equal", [P, 2, N], BF16)
        ranked = sb("ranked", [P, 2, N], BF16)
        best = sb("best", [P, 2, T], BF16)
        onehot = sb("onehot", [P, 2, N], BF16)
        oh_out = sb("oh_out", [P, 2, NT, P], F32R)
        total, mean_c, sq_c, var_c, std_c, rstd_c, neg_c = (col[:, i:i + 1] for i in range(7))

        prod = psum("prod", [P, BANKS, HALF])
        turned = psum("turned", [P, 2, HALF])
        stat = psum("stat", [P, HALF])
        oh_ps = psum("oh_ps", [P, NT, P], BF16)

        consts = sem("consts")
        c_loaded = sem("c_loaded")
        w_high = sem("w_high")
        w_low = sem("w_low")
        o_loaded = sem("o_loaded")
        x_loaded = sem("x_loaded")
        o_high = sem("o_high")
        o_low = sem("o_low")
        x_beta = sem("x_beta")
        prod_full = sem("prod_full")
        y_done = sem("y_done")
        totals = sem("totals")
        averaged = sem("averaged")
        centre = sem("centre")
        squared = sem("squared")
        std_in = sem("std_in")
        std_out = sem("std_out")
        mid_done = sem("mid_done")
        colsum = sem("colsum")
        centred = sem("centred")
        dev_sq = sem("dev_sq")
        grstd_done = sem("grstd_done")
        feat_even = sem("feat_even")
        feat_odd = sem("feat_odd")
        norm_sq = sem("norm_sq")
        unit = sem("unit")
        turn_full = sem("turn_full")
        high_done = sem("high_done")
        low_done = sem("low_done")
        sim_full = sem("sim_full")
        eq_done = sem("eq_done")
        rank_done = sem("rank_done")
        best_top = sem("best_top")
        best_done = sem("best_done")
        hot_done = sem("hot_done")
        hot_turned = sem("hot_turned")
        hot_out = sem("hot_out")
        dchain = sem("dchain")
        mid_stored = sem("mid_stored")
        feat_stored = sem("feat_stored")
        hot_stored = [sem("hot_stored0"), sem("hot_stored1")]
        block = ctx.enter_context(nc.Block())

        def per_group(v):
            return v.unsqueeze(2).to_broadcast([P, NG, GROUP])

        @block.sync
        def _(sp):
            att = attended.rearrange("g i d -> (g i d)").rearrange("(r n) -> r n", n=N)
            load_o = lambda b: sp.dma_start(o_raw[:], att[bass.ds(b * C, C), :].rearrange("(k p) n -> p k n", p=P)
                                            ).then_inc(o_loaded, 16)
            load_x = lambda b: sp.dma_start(x_tok[:], x[bass.ds(b * N, N), :].rearrange("(t p) c -> p t c", p=P)
                                            ).then_inc(x_loaded, 16)
            load_o(0)
            sp.dma_start(w_raw[:], w_out.rearrange("(k p) c -> p k c", p=P)).then_inc(c_loaded, 16)
            load_x(0)
            for row, src in ((bias, b_out), (gam, gamma), (bet, beta)):
                sp.dma_start(row[:], src.partition_broadcast(P)).then_inc(c_loaded, 16)
            with nc.allow_non_contiguous_dma("512 numbers of a diagonal, once"):
                sp.dma_start(diag[:], w_diag).then_inc(c_loaded, 16)
            sp.sem_inc(feat_stored, 16)
            for h in hot_stored:
                sp.sem_inc(h, 16)

            def batch(b, last):
                if not last:
                    sp.wait_ge(o_low, b * KC + KC)
                    load_o(b + 1)
                sp.wait_ge(mid_done, b + 1)
                sp.dma_start(x_mid[bass.ds(b * N, N), :].rearrange("(t p) c -> p t c", p=P), x_tok[:]
                             ).then_inc(mid_stored, 16)
                if not last:
                    sp.wait_ge(mid_stored, b * 16 + 16)
                    sp.wait_ge(centred, b * NT + NT)
                    load_x(b + 1)
                sp.wait_ge(feat_even, b * (NT // 2) + NT // 2)
                sp.wait_ge(feat_odd, b * (NT // 2) + NT // 2)
                sp.dma_start(feat_rows[bass.ds(b * N, N), :].rearrange("(t p) c -> p t c", p=P), y[:]
                             ).then_inc(feat_stored, 16)
                for t in range(NT):
                    sp.wait_ge(hot_out, 1 + b * NT + t + 1)
                    sp.dma_start(chosen[bass.ds(b * N, N), t * P:(t + 1) * P].rearrange("(j p) n -> p j n", p=P),
                                 oh_out[:, t % 2].bitcast(F32)).then_inc(hot_stored[t % 2], 16)

            with sp.Fori(0, B - 1) as b:
                batch(b, False)
            batch(B - 1, True)
            sp.wait_ge(mid_stored, 16 * B)
            sp.wait_ge(feat_stored, 16 + 16 * B)
            for h in hot_stored:
                sp.wait_ge(h, 16 + 16 * B * NT // 2)

        @block.gpsimd
        def _(pool):
            n = 0
            for ins in (lambda: pool.memset(ident[:], 0.0),
                        lambda: pool.memset(all_avg[:], 1.0 / (N * C)),
                        lambda: pool.memset(grp_avg[:], 1.0 / (N * GROUP)),
                        lambda: pool.affine_select(out=ident[:], in_=ident[:], compare_op=ALU.not_equal, fill=1.0,
                                                   base=0, pattern=[[-1, P]], channel_multiplier=1),
                        lambda: pool.tensor_copy(ident_b[:], ident[:]),
                        lambda: pool.iota(ramp[:], pattern=[[-1, M]], base=M, channel_multiplier=0,
                                          allow_small_or_imprecise_dtypes=True)):
                ins().then_inc(consts, 1)
                n += 1
                pool.wait_ge(consts, n)
            pool.wait_ge(c_loaded, 16 * 5)
            with pool.Fori(0, B) as b:
                for k in range(KC):
                    pool.wait_ge(o_high, b * KC + k + 1)
                    pool.tensor_tensor(n_l[:, k, :], o_raw[:, k, :], n_h[:, k, :].bitcast(F32),
                                       ALU.subtract).then_inc(o_low, 1)
                pool.wait_ge(x_loaded, b * 16 + 16)
                pool.tensor_tensor(x_tok[:], x_tok[:], bet[:].unsqueeze(1).to_broadcast([P, NT, C]),
                                   ALU.add).then_inc(x_beta, 1)
                for t in range(1, NT, 2):
                    if t == 1:
                        pool.wait_ge(grstd_done, b + 1)
                    tile = y[:, t, :].rearrange("p (g c) -> p g c", c=GROUP)
                    pool.tensor_tensor(tile, tile, per_group(grstd[:]), ALU.mult).then_inc(feat_odd, 1)
                ranks = ramp[:].unsqueeze(1).to_broadcast([P, T, M])
                for t in range(NT):
                    pool.wait_ge(eq_done, b * NT + t + 1)
                    if t >= 2:
                        pool.wait_ge(hot_done, b * NT + t - 1)
                    pool.tensor_tensor(ranked[:, t % 2, :].rearrange("p (t m) -> p t m", m=M),
                                       equal[:, t % 2, :].rearrange("p (t m) -> p t m", m=M),
                                       ranks, ALU.mult).then_inc(rank_done, 1)

        @block.scalar
        def _(act):
            act.sem_inc(hot_out, 1)
            act.wait_ge(c_loaded, 16 * 5)
            for k in range(KC):
                act.activation(w_h[:, k, :], w_raw[:, k, :], ACT.Copy).then_inc(w_high, 1)
            with act.Fori(0, B) as b:
                act.wait_ge(o_loaded, b * 16 + 16)
                for k in range(KC):
                    act.activation(n_h[:, k, :], o_raw[:, k, :], ACT.Copy).then_inc(o_high, 1)
                act.wait_ge(centre, b + 1)
                for t in range(NT):
                    act.activation(work[:, t, :], y[:, t, :], ACT.Square, bias=neg_c,
                                   accum_out=ysq[:, t:t + 1]).then_inc(squared, 1)
                act.wait_ge(std_in, b * 2 + 1)
                act.activation(std_c, var_c, ACT.Sqrt).then_inc(std_out, 1)
                for t in range(NT):
                    act.wait_ge(centred, b * NT + t + 1)
                    act.activation(work[:, t, :], y[:, t, :], ACT.Square).then_inc(dev_sq, 1)
                act.wait_ge(std_in, b * 2 + 2)
                act.activation(gstd[:], gvar[:], ACT.Sqrt).then_inc(std_out, 1)
                for t in range(NT):
                    act.wait_ge((feat_even, feat_odd)[t % 2], b * (NT // 2) + t // 2 + 1)
                    act.activation(work[:, t, :], y[:, t, :], ACT.Square,
                                   accum_out=nsq[:, t:t + 1]).then_inc(norm_sq, 1)
                act.wait_ge(norm_sq, b * NT + NT)
                act.activation(nstd[:], nsq[:], ACT.Sqrt).then_inc(std_out, 1)
                for g in range(2 * KC):
                    cols = slice(g % 2 * HALF, (g % 2 + 1) * HALF)
                    act.wait_ge(turn_full, b * 2 * KC + g + 1)
                    act.activation(n_h[:, g // 2, cols], turned[:, g % 2, :], ACT.Copy).then_inc(high_done, 1)
                    act.activation(m_h[:, g // 2, cols], turned[:, g % 2, :], ACT.Copy,
                                   scale=diag[:, g // 2:g // 2 + 1]).then_inc(high_done, 1)
                for t in range(NT):
                    act.wait_ge(hot_stored[t % 2], 16 + b * 16 * (NT // 2) + t // 2 * 16)
                    act.wait_ge(hot_turned, b * NT + t + 1)
                    act.activation(oh_out[:, t % 2], oh_ps[:], ACT.Copy).then_inc(hot_out, 1)

        @block.vector
        def _(dve):
            dve.sem_inc(y_done, BANKS)
            dve.sem_inc(low_done, 2)
            for k in range(KC):
                dve.wait_ge(w_high, k + 1)
                dve.tensor_tensor(w_l[:, k, :], w_raw[:, k, :], w_h[:, k, :].bitcast(F32),
                                  ALU.subtract).then_inc(w_low, 1)
            with dve.Fori(0, B) as b:
                link = Chain(dve, dchain, b * DCHAIN)
                dve.wait_ge(feat_stored, 16 + b * 16)
                for t in range(NT):
                    dve.wait_ge(prod_full, b * NT + t + 1)
                    dve.scalar_tensor_tensor(y[:, t, :], prod[:, t % BANKS, :], 1.0, bias[:], ALU.mult, ALU.add,
                                             accum_out=ysum[:, t:t + 1]).then_inc(y_done, 1)
                dve.wait_ge(y_done, BANKS + b * NT + NT)
                dve.tensor_reduce(total, ysum[:], AX.X, ALU.add).then_inc(totals, 1)
                dve.wait_ge(averaged, b * 2 + 1)
                link(dve.tensor_copy(mean_c, stat[:, 0:1]))
                dve.tensor_scalar(neg_c, mean_c, -1.0, None, ALU.mult).then_inc(centre, 1)
                dve.wait_ge(squared, b * NT + NT)
                dve.tensor_reduce(sq_c, ysq[:], AX.X, ALU.add).then_inc(totals, 1)
                dve.wait_ge(averaged, b * 2 + 2)
                dve.tensor_scalar(var_c, stat[:, 1:2], GN_OUT_EPS, None, ALU.add).then_inc(std_in, 1)
                dve.wait_ge(std_out, b * 3 + 1)
                link(dve.reciprocal(rstd_c, std_c))
                link(dve.tensor_scalar(gam_r[:], gam[:], rstd_c, None, ALU.mult))
                link(dve.scalar_tensor_tensor(y[:], y[:], mean_c, gam_r[:].unsqueeze(1).to_broadcast([P, NT, C]),
                                              ALU.subtract, ALU.mult))
                dve.wait_ge(x_beta, b + 1)
                dve.tensor_tensor(x_tok[:], x_tok[:], y[:], ALU.add).then_inc(mid_done, 1)
                dve.wait_ge(colsum, b * 2 + 1)
                link(dve.tensor_reduce(gmean[:], stat[:].rearrange("p (g c) -> p g c", c=GROUP), AX.X, ALU.add))
                for t in range(NT):
                    dve.tensor_tensor(y[:, t, :].rearrange("p (g c) -> p g c", c=GROUP),
                                      x_tok[:, t, :].rearrange("p (g c) -> p g c", c=GROUP),
                                      per_group(gmean[:]), ALU.subtract).then_inc(centred, 1)
                dve.wait_ge(colsum, b * 2 + 2)
                link(dve.tensor_reduce(gvar[:], stat[:].rearrange("p (g c) -> p g c", c=GROUP), AX.X, ALU.add))
                dve.tensor_scalar(gvar[:], gvar[:], GN_IN_EPS, None, ALU.add).then_inc(std_in, 1)
                dve.wait_ge(std_out, b * 3 + 2)
                dve.reciprocal(grstd[:], gstd[:]).then_inc(grstd_done, 1)
                dve.wait_ge(grstd_done, b + 1)
                for t in range(0, NT, 2):
                    tile = y[:, t, :].rearrange("p (g c) -> p g c", c=GROUP)
                    dve.tensor_tensor(tile, tile, per_group(grstd[:]), ALU.mult).then_inc(feat_even, 1)
                dve.wait_ge(std_out, b * 3 + 3)
                link(dve.tensor_scalar(nstd[:], nstd[:], 1e-12, None, ALU.max))
                link(dve.reciprocal(nrec[:], nstd[:]))
                for t in range(NT):
                    dve.tensor_scalar(work[:, t, :], y[:, t, :], nrec[:, t:t + 1], None, ALU.mult).then_inc(unit, 1)
                for g in range(2 * KC):
                    cols = slice(g % 2 * HALF, (g % 2 + 1) * HALF)
                    dve.wait_ge(high_done, b * 4 * KC + 2 * g + 2)
                    dve.tensor_tensor(n_l[:, g // 2, cols], turned[:, g % 2, :],
                                      n_h[:, g // 2, cols].bitcast(F32), ALU.subtract)
                    dve.scalar_tensor_tensor(m_l[:, g // 2, cols], turned[:, g % 2, :], diag[:, g // 2:g // 2 + 1],
                                             m_h[:, g // 2, cols].bitcast(F32), ALU.mult,
                                             ALU.subtract).then_inc(low_done, 1)
                for t in range(NT + 1):
                    if t < NT:
                        sims = prod[:, t % 2 * 2:t % 2 * 2 + 2, :].rearrange("p h (t m) -> p (h t) m", m=M)
                        dve.wait_ge(sim_full, b * NT + t + 1)
                        dve.tensor_reduce(top[:, t % 2, :], sims, AX.X, ALU.max).then_inc(best_top, 1)
                        if t >= 2:
                            dve.wait_ge(rank_done, b * NT + t - 1)
                        dve.wait_ge(best_top, b * NT + t + 1)
                        dve.tensor_tensor(equal[:, t % 2, :].rearrange("p (t m) -> p t m", m=M), sims,
                                          top[:, t % 2, :].unsqueeze(2).to_broadcast([P, T, M]),
                                          ALU.is_equal).then_inc(eq_done, 1)
                    if t > 0:
                        u = t - 1
                        dve.wait_ge(rank_done, b * NT + u + 1)
                        dve.tensor_reduce(best[:, u % 2, :], ranked[:, u % 2, :].rearrange("p (t m) -> p t m", m=M),
                                          AX.X, ALU.max).then_inc(best_done, 1)
                        dve.wait_ge(best_done, b * NT + u + 1)
                        if u >= 2:
                            dve.wait_ge(hot_turned, b * NT + u - 1)
                        dve.tensor_tensor(onehot[:, u % 2, :].rearrange("p (t m) -> p t m", m=M),
                                          ranked[:, u % 2, :].rearrange("p (t m) -> p t m", m=M),
                                          best[:, u % 2, :].unsqueeze(2).to_broadcast([P, T, M]),
                                          ALU.is_equal).then_inc(hot_done, 1)
                assert link.n == DCHAIN, link.n

        @block.tensor
        def _(pe):
            def turn_hot(b, u):
                pe.wait_ge(hot_done, b * NT + u + 1)
                pe.wait_ge(hot_out, b * NT + u + 1)
                for j in range(NT):
                    ins = pe.transpose(oh_ps[:, j, :], onehot[:, u % 2, j * P:(j + 1) * P], ident_b[:])
                ins.then_inc(hot_turned, 1)

            pe.wait_ge(consts, 6)
            pe.wait_ge(w_low, KC)
            with pe.Fori(0, B) as b:
                pe.wait_ge(o_low, b * KC + KC)
                for t in range(NT):
                    pe.wait_ge(y_done, b * NT + t + 1)
                    for n, (o, w) in enumerate(((n_h, w_h), (n_h, w_l), (n_l, w_h))):
                        for k in range(KC):
                            ins = pe.matmul(prod[:, t % BANKS, :], o[:, k, t * P:(t + 1) * P], w[:, k, :],
                                            start=n == 0 and k == 0, stop=n == 2 and k == KC - 1)
                    ins.then_inc(prod_full, 1)
                pe.wait_ge(totals, b * 2 + 1)
                pe.matmul(stat[:, 0:1], all_avg[:], total, start=True, stop=True).then_inc(averaged, 1)
                pe.wait_ge(totals, b * 2 + 2)
                pe.matmul(stat[:, 1:2], all_avg[:], sq_c, start=True, stop=True).then_inc(averaged, 1)
                pe.wait_ge(mid_done, b + 1)
                for t in range(NT):
                    ins = pe.matmul(stat[:], grp_avg[:], x_tok[:, t, :], start=t == 0, stop=t == NT - 1)
                ins.then_inc(colsum, 1)
                for t in range(NT):
                    pe.wait_ge(dev_sq, b * NT + t + 1)
                    ins = pe.matmul(stat[:], grp_avg[:], work[:, t, :], start=t == 0, stop=t == NT - 1)
                ins.then_inc(colsum, 1)
                for g in range(2 * KC):
                    pe.wait_ge(unit, b * NT + NT)
                    pe.wait_ge(low_done, b * 2 * KC + g + 1)
                    for j in range(4):
                        t = g % 2 * 4 + j
                        ins = pe.transpose(turned[:, g % 2, j * P:(j + 1) * P],
                                           work[:, t, g // 2 * P:(g // 2 + 1) * P], ident[:])
                    ins.then_inc(turn_full, 1)
                pe.wait_ge(low_done, 2 + b * 2 * KC + 2 * KC)
                for t in range(NT):
                    if t >= 2:
                        pe.wait_ge(eq_done, b * NT + t - 1)
                    for h in range(2):
                        for n, (m, u) in enumerate(((m_h, n_h), (m_h, n_l), (m_l, n_h))):
                            for k in range(KC):
                                ins = pe.matmul(prod[:, t % 2 * 2 + h, :], m[:, k, t * P:(t + 1) * P],
                                                u[:, k, h * HALF:(h + 1) * HALF],
                                                start=n == 0 and k == 0, stop=n == 2 and k == KC - 1)
                    ins.then_inc(sim_full, 1)
                    if t >= 2:
                        turn_hot(b, t - 2)
                turn_hot(b, NT - 2)
                turn_hot(b, NT - 1)


def convolution_phase(nc, chosen, feat_rows, x_mid, conv_w, conv_b, gamma, beta, out):
    LEAK = 0.01
    TINY = 2.0 ** -60
    ROWS = (P, (KS - P // M) * M)
    STEPS = B * TO
    SETUP = 30
    BANKS = 4
    with ExitStack() as ctx:
        def sb(name, shape, dt=F32):
            return ctx.enter_context(nc.sbuf_tensor("p4_" + name, shape, dt))

        def psum(name, shape, dt=F32):
            return ctx.enter_context(nc.psum_tensor("p4_" + name, shape, dt))

        def sem(name):
            return ctx.enter_context(nc.semaphore("p4_" + name))

        ident = sb("ident", [P, P])
        pick = sb("pick", [8, 2, P])
        w_raw = sb("w_raw", [P, KC, KS])
        w_t = sb("w_t", [8, C])
        taps = sb("taps", [P, 2, C])
        b_row = sb("b_row", [P, C])
        b_col = sb("b_col", [P, 2])
        gam = sb("gam", [P, C])
        bet = sb("bet", [P, C])
        size = sb("size", [P, C])
        sign = sb("sign", [P, C])
        shift = sb("shift", [P, C])
        c_lin = sb("c_lin", [P, C])
        c_abs = sb("c_abs", [P, C])
        win = sb("win", [P, 2, 2, N], F32R)
        blocks = sb("blocks", [P, P // M])
        spot = sb("spot", [P, M])
        high_spot = sb("high_spot", [P, BANKS])
        low_spot = sb("low_spot", [P, BANKS])
        shift_h = sb("shift_h", [P, C], F32R)
        shift_l = sb("shift_l", [P, C], F32R)
        shift_rows = sb("shift_rows", [P, BANKS, C], F32R)
        parts = sb("parts", [P, 2, M], F32R)
        parts_t = sb("parts_t", [P, 2, M])
        level = sb("level", [P, 2, P], F32R)
        f_win = sb("f_win", [P, 2, 2, C])
        tapped = sb("tapped", [P, 2, 2, C])
        tap_sum = sb("tap_sum", [P, 2, 2])
        tap_mean = sb("tap_mean", [P, 2, 2])
        g_h = sb("g_h", [P, 2, 2, C], F32R)
        g_l = sb("g_l", [P, 2, 2, C], F32R)
        junk = sb("junk", [P, BANKS, C])
        sq = sb("sq", [P, 2, BANKS])
        var = sb("var", [P, 2, BANKS])
        std = sb("std", [P, 2, BANKS])
        rstd = sb("rstd", [P, 2, BANKS])
        size_d = sb("size_d", [P, 2, BANKS, C])
        sum_d = sb("sum_d", [P, NT, C])
        sum_abs = sb("sum_abs", [P, NT, C])
        mid = sb("mid", [P, NT, C])
        bank = psum("bank", [P, 2, BANKS, C])

        consts = sem("consts")
        c_loaded = sem("c_loaded")
        setup = sem("setup")
        ones_done = sem("ones_done")
        w_turned = sem("w_turned")
        taps_full = sem("taps_full")
        bias_high = sem("bias_high")
        win_loaded = [sem("win_loaded0"), sem("win_loaded1")]
        f_loaded = [sem("f_loaded0"), sem("f_loaded1")]
        tap_done = sem("tap_done")
        mean_done = sem("mean_done")
        high_done = sem("high_done")
        low_done = sem("low_done")
        conv_full = sem("conv_full")
        squared = sem("squared")
        var_done = sem("var_done")
        std_done = sem("std_done")
        parts_done = sem("parts_done")
        level_done = sem("level_done")
        shifted = sem("shifted")
        abs_done = sem("abs_done")
        lin_added = sem("lin_added")
        abs_added = sem("abs_added")
        mid_loaded = sem("mid_loaded")
        abs_scaled = sem("abs_scaled")
        dchain = sem("dchain")
        finished = sem("finished")
        stored = sem("stored")
        block = ctx.enter_context(nc.Block())

        def batches(engine, step, flush):
            with engine.Fori(0, B) as b:
                for k in range(2):
                    step(b, k, k, True)
                with engine.Fori(1, TO // 2) as pair:
                    for k in range(2):
                        step(b, pair * 2 + k, k, False)
                flush(b)

        def before(f, g, first):
            return (0, 0) if g == 1 else None if first and f == 0 else (-1, 1)

        @block.sync
        def _(sp):
            with nc.allow_non_contiguous_dma("taps of a channel, once"):
                sp.dma_start(w_raw[:], conv_w.rearrange("(k p) o t -> p k (o t)", p=P)).then_inc(c_loaded, 16)
            sp.dma_start(b_row[96:97, :], conv_b.unsqueeze(0)).then_inc(c_loaded, 16)
            for row, src in ((gam, gamma), (bet, beta)):
                sp.dma_start(row[:], src.partition_broadcast(P)).then_inc(c_loaded, 16)

            def load_features(row, k):
                for c in range(2):
                    sp.dma_start(f_win[0:ROWS[c], k, c, :], feat_rows[bass.ds(row + c * P, ROWS[c]), :]
                                 ).then_inc(f_loaded[k], 16)

            def frame(b, f, k, ahead):
                v = b * TO + f
                sp.wait_ge(tap_done, 2 * v + 2)
                load_features(ahead, k)
                sp.wait_ge(conv_full, NT * v + NT)
                for c in range(2):
                    sp.dma_start(win[0:ROWS[c], k, c, :].bitcast(F32),
                                 chosen[bass.ds(b * N + f * M + c * P, ROWS[c]), :]).then_inc(win_loaded[k], 16)

            def batch(b, first, last):
                for k in range(2):
                    frame(b, k, k, b * N + (2 + k) * M)
                if not first:
                    sp.wait_ge(finished, 2 * b + 2)
                    sp.dma_start(out[bass.ds(b * N - N, N), :].rearrange("(t p) c -> p t c", p=P), mid[:]
                                 ).then_inc(stored, 16)
                    sp.wait_ge(stored, b * 16)
                sp.dma_start(mid[:], x_mid[bass.ds(b * N, N), :].rearrange("(t p) c -> p t c", p=P)
                             ).then_inc(mid_loaded, 16)
                with sp.Fori(1, TO // 2 - 1) as pair:
                    for k in range(2):
                        frame(b, pair * 2 + k, k, b * N + (pair * 2 + k + 2) * M)
                for k in range(2):
                    frame(b, TO - 2 + k, k, k * M if last else b * N + N + k * M)

            for k in range(2):
                load_features(k * M, k)
            batch(0, True, False)
            with sp.Fori(1, B - 1) as b:
                batch(b, False, False)
            batch(B - 1, False, True)
            sp.wait_ge(finished, 2 * B + 2)
            sp.dma_start(out[B * N - N:B * N, :].rearrange("(t p) c -> p t c", p=P), mid[:]).then_inc(stored, 16)
            sp.wait_ge(stored, B * 16)

        @block.gpsimd
        def _(pool):
            pool.memset(ident[:], 0.0).then_inc(consts, 1)
            pool.wait_ge(consts, 1)
            pool.memset(pick[:], 0.0).then_inc(consts, 1)
            pool.wait_ge(consts, 2)
            pool.affine_select(out=ident[:], in_=ident[:], compare_op=ALU.not_equal, fill=1.0, base=0,
                               pattern=[[-1, P]], channel_multiplier=1).then_inc(consts, 1)
            pool.wait_ge(consts, 3)
            spots = pick[:].rearrange("k c (f m) -> k c f m", m=M)
            pool.affine_select(out=spots, in_=spots, compare_op=ALU.not_equal, fill=1.0, base=0,
                               pattern=[[-P // M, 2], [-1, P // M], [0, M]], channel_multiplier=1).then_inc(consts, 1)

            def add(b, v, g):
                pool.wait_ge(abs_done, BANKS * (2 * v + g + 1))
                cols = slice(g * BANKS, (g + 1) * BANKS)
                pool.tensor_tensor(sum_abs[:, cols, :], sum_abs[:, cols, :], size_d[:, g], ALU.add
                                   ).then_inc(abs_added, 1)

            def step(b, f, k, first):
                v = b * TO + f
                for g in range(2):
                    was = before(f, g, first)
                    if was and not (first and f + was[0] == 0):
                        add(b, v + was[0], was[1])

            def flush(b):
                add(b, b * TO + TO - 1, 1)
                for g in range(2):
                    pool.wait_ge(abs_added, 1 + (b + 1) * 2 * (TO - 1) - 1 + g)
                    cols = slice(g * BANKS, (g + 1) * BANKS)
                    pool.tensor_tensor(sum_abs[:, cols, :], sum_abs[:, cols, :],
                                       c_abs[:].unsqueeze(1).to_broadcast([P, BANKS, C]),
                                       ALU.mult).then_inc(abs_scaled, 1)

            pool.sem_inc(abs_added, 1)
            pool.wait_ge(setup, SETUP)
            batches(pool, step, flush)

        @block.scalar
        def _(act):
            def high(w, k):
                act.wait_ge(mean_done, w + 1)
                for c in range(2):
                    rows = slice(0, ROWS[c])
                    act.activation(g_h[rows, k, c, :], tapped[rows, k, c, :], ACT.Identity,
                                   bias=tap_mean[rows, k, c:c + 1]).then_inc(high_done, 1)

            def square(q, g, j):
                act.wait_ge(conv_full, 2 * NT + BANKS * q + j + 1)
                act.activation(junk[:, j, :], bank[:, g, j, :], ACT.Square,
                               accum_out=sq[:, g, j:j + 1]).then_inc(squared, 1)

            def absolute(b, f, g, j, begins, reused):
                q = 2 * (b * TO + f) + g
                if begins:
                    act.wait_ge(finished, 2 * b + g + 1)
                    to = sum_abs[:, g * BANKS + j, :]
                else:
                    if reused:
                        act.wait_ge(abs_added, 1 + b * 2 * (TO - 1) + f * 2 - 3 + g)
                    to = size_d[:, g, j, :]
                act.wait_ge(shifted, BANKS * q + j + 1)
                act.activation(to, bank[:, g, j, :], ACT.Abs, scale=rstd[:, g, j:j + 1]).then_inc(abs_done, 1)

            def step(b, f, k, first):
                v = b * TO + f
                for g in range(2):
                    q = 2 * v + g
                    was = before(f, g, first)

                    def last(*js):
                        for j in js:
                            if was:
                                absolute(b, f + was[0], was[1], j, first and f + was[0] == 0,
                                         not (first and f + was[0] < 2))

                    square(q, g, 0)
                    square(q, g, 1)
                    last(0)
                    square(q, g, 2)
                    last(1)
                    square(q, g, 3)
                    last(2)
                    act.wait_ge(var_done, q + 1)
                    act.activation(std[:, g, :], var[:, g, :], ACT.Sqrt).then_inc(std_done, 1)
                    last(3)
                    if g == 0:
                        high(v + 1, 1 - k)

            def flush(b):
                for j in range(BANKS):
                    absolute(b, TO - 1, 1, j, False, True)

            act.wait_ge(setup, 2)
            for k in range(2):
                act.activation(g_h[96:97, k, 1, :], b_row[96:97, :], ACT.Identity, bias=b_col[96:97, 1:2]
                               ).then_inc(bias_high, 1)
            high(0, 0)
            batches(act, step, flush)

        @block.vector
        def _(dve):
            done = Chain(dve, setup, 0)
            dve.memset(win[96:97, :, 1, :].bitcast(F32), 1.0).then_inc(ones_done, 1)
            dve.memset(tap_sum[:], 0.0).then_inc(ones_done, 1)
            dve.wait_ge(c_loaded, 64)
            done(dve.tensor_reduce(b_col[96:97, 0:1], b_row[96:97, :], AX.X, ALU.add))
            done(dve.tensor_scalar(b_col[96:97, 1:2], b_col[96:97, 0:1], -1.0 / C, None, ALU.mult))
            dve.wait_ge(bias_high, 2)
            for k in range(2):
                done(dve.scalar_tensor_tensor(g_l[96:97, k, 1, :], b_row[96:97, :], b_col[96:97, 1:2],
                                              g_h[96:97, k, 1, :].bitcast(F32), ALU.add, ALU.subtract))
            dve.wait_ge(w_turned, 1)
            done(dve.tensor_copy(w_t[0:KS, :], bank[0:KS, 0, 0, :]))
            dve.wait_ge(taps_full, 1)
            done(dve.tensor_copy(taps[:], bank[:, 0, 1:3, :]))
            done(dve.scalar_tensor_tensor(size[:], gam[:], -1.0, gam[:], ALU.mult, ALU.max))
            done(dve.tensor_scalar(size[:], size[:], TINY, None, ALU.max))
            done(dve.tensor_scalar(sign[:], gam[:], 0.0, 2.0, ALU.is_ge, ALU.mult))
            done(dve.tensor_scalar(sign[:], sign[:], -1.0, None, ALU.add))
            done(dve.tensor_tensor(c_lin[:], size[:], sign[:], ALU.mult))
            done(dve.reciprocal(shift[:], c_lin[:]))
            done(dve.tensor_tensor(shift[:], shift[:], bet[:], ALU.mult))
            done(dve.tensor_copy(shift_h[:], shift[:]))
            done(dve.tensor_tensor(shift_l[:], shift[:], shift_h[:].bitcast(F32), ALU.subtract))
            done(dve.tensor_reduce(blocks[:], ident[:].rearrange("p (a i) -> p a i", i=M), AX.X, ALU.add))
            done(dve.tensor_reduce(spot[:], ident[:].rearrange("p (a i) -> p i a", i=M), AX.X, ALU.add))
            three = spot[:, 0:3 * BANKS].rearrange("p (j r) -> p j r", r=3)
            done(dve.tensor_tensor(high_spot[:].unsqueeze(2), three[:, :, 0:1], three[:, :, 2:3], ALU.add))
            done(dve.tensor_copy(low_spot[:].unsqueeze(2), three[:, :, 1:2]))
            for j in range(BANKS):
                done(dve.tensor_scalar(junk[:, j, :], shift_l[:].bitcast(F32), low_spot[:, j:j + 1], None, ALU.mult))
                done(dve.scalar_tensor_tensor(shift_rows[:, j, :], shift_h[:].bitcast(F32), high_spot[:, j:j + 1],
                                              junk[:, j, :], ALU.mult, ALU.add))
            done(dve.memset(parts[:].bitcast(F32), 0.0))
            done(dve.tensor_scalar(c_lin[:], c_lin[:], 0.5 * (1.0 + LEAK) / TO, None, ALU.mult))
            done(dve.tensor_scalar(c_abs[:], size[:], 0.5 * (1.0 - LEAK) / TO, None, ALU.mult))
            assert done.n == SETUP, done.n

            def tap(w, k):
                dve.wait_ge(f_loaded[k], (w - k) * 16 + 32)
                for c in range(2):
                    rows = slice(0, ROWS[c])
                    dve.scalar_tensor_tensor(tapped[rows, k, c, :], f_win[rows, k, c, :], 1.0, taps[rows, c, :],
                                             ALU.mult, ALU.mult,
                                             accum_out=tap_sum[rows, k, c:c + 1]).then_inc(tap_done, 1)
                dve.wait_ge(tap_done, 2 * w + 2)
                dve.tensor_scalar(tap_mean[:, k, :], tap_sum[:, k, :], -1.0 / C, None, ALU.mult
                                  ).then_inc(mean_done, 1)

            def low(w, k):
                for c in range(2):
                    rows = slice(0, ROWS[c])
                    dve.wait_ge(high_done, 2 * w + c + 1)
                    ins = dve.scalar_tensor_tensor(g_l[rows, k, c, :], tapped[rows, k, c, :],
                                                   tap_mean[rows, k, c:c + 1], g_h[rows, k, c, :].bitcast(F32),
                                                   ALU.add, ALU.subtract)
                ins.then_inc(low_done, 1)

            def add(v, g, j, begins):
                bank_no = BANKS * (2 * v + g) + j
                dve.wait_ge(abs_done, bank_no + 1)
                total = sum_d[:, g * BANKS + j, :]
                if begins:
                    ins = dve.tensor_scalar(total, bank[:, g, j, :], rstd[:, g, j:j + 1], None, ALU.mult)
                else:
                    dve.wait_ge(lin_added, bank_no + 1)
                    ins = dve.scalar_tensor_tensor(total, bank[:, g, j, :], rstd[:, g, j:j + 1], total,
                                                   ALU.mult, ALU.add)
                ins.then_inc(lin_added, 1)

            def level_rows(q, g):
                dve.wait_ge(std_done, q + 1)
                dve.reciprocal(rstd[:, g, :], std[:, g, :]).then_inc(parts_done, 1)
                three = parts[:, g, 0:3 * BANKS].rearrange("p (j r) -> p j r", r=3)
                column = std[:, g, :].unsqueeze(2)
                dve.tensor_copy(three[:, :, 0:2], column.to_broadcast([P, BANKS, 2])).then_inc(parts_done, 1)
                dve.wait_ge(parts_done, 4 * q + 2)
                dve.tensor_tensor(three[:, :, 2:3], column, three[:, :, 0:1].bitcast(F32), ALU.subtract
                                  ).then_inc(parts_done, 1)
                dve.wait_ge(parts_done, 4 * q + 3)
                dve.transpose(parts_t[:, g, :], parts[:, g, :].bitcast(F32)).then_inc(parts_done, 1)
                dve.wait_ge(parts_done, 4 * q + 4)
                dve.tensor_tensor(level[:, g, :].rearrange("p (a i) -> p a i", i=M),
                                  parts_t[:, g, :].unsqueeze(1).to_broadcast([P, P // M, M]),
                                  blocks[:].unsqueeze(2).to_broadcast([P, P // M, M]), ALU.mult
                                  ).then_inc(level_done, 1)

            def step(b, f, k, first):
                v = b * TO + f
                for g in range(2):
                    q = 2 * v + g
                    was = before(f, g, first)

                    def last(*js):
                        for j in js:
                            if was:
                                add(v + was[0], was[1], j, first and f + was[0] == 0)

                    last(0, 1)
                    dve.wait_ge(squared, BANKS * (q + 1))
                    dve.tensor_scalar(var[:, g, :], sq[:, g, :], 1.0 / C, LN_EPS, ALU.mult, ALU.add
                                      ).then_inc(var_done, 1)
                    last(2)
                    level_rows(q, g)
                    last(3)
                    if g == 0:
                        low(v + 1, 1 - k)
                    else:
                        tap(v + 2, k)

            def flush(b):
                for j in range(BANKS):
                    add(b * TO + TO - 1, 1, j, False)
                dve.wait_ge(mid_loaded, b * 16 + 16)
                link = Chain(dve, dchain, b * 4)
                for g in range(2):
                    cols = slice(g * BANKS, (g + 1) * BANKS)
                    dve.wait_ge(lin_added, (b + 1) * TO * NT + (g + 1) * BANKS)
                    link(dve.tensor_tensor(sum_d[:, cols, :], sum_d[:, cols, :],
                                           c_lin[:].unsqueeze(1).to_broadcast([P, BANKS, C]), ALU.mult))
                    link(dve.tensor_tensor(mid[:, cols, :], mid[:, cols, :], sum_d[:, cols, :], ALU.add))
                    dve.wait_ge(abs_scaled, b * 2 + g + 1)
                    dve.tensor_tensor(mid[:, cols, :], mid[:, cols, :], sum_abs[:, cols, :], ALU.add
                                      ).then_inc(finished, 1)

            dve.sem_inc(lin_added, 2 * BANKS)
            dve.sem_inc(finished, 2)
            tap(0, 0)
            low(0, 0)
            tap(1, 1)
            batches(dve, step, flush)

        @block.tensor
        def _(pe):
            pe.sem_inc(conv_full, 2 * NT)
            pe.wait_ge(consts, 4)
            pe.wait_ge(c_loaded, 64)
            for k in range(KC):
                ins = pe.transpose(bank[0:KS, 0, 0, k * P:(k + 1) * P], w_raw[:, k, :], ident[:])
            ins.then_inc(w_turned, 1)
            pe.wait_ge(setup, 5)
            for c in range(2):
                ins = pe.matmul(bank[:, 0, 1 + c, :], pick[0:KS, c, :], w_t[0:KS, :], start=True, stop=True)
            ins.then_inc(taps_full, 1)
            pe.wait_ge(ones_done, 2)
            pe.wait_ge(setup, SETUP)

            def fill(v, k, g, j):
                pe.wait_ge(low_done, v + 1)
                pe.wait_ge(win_loaded[k], (v - k) * 16 + 32)
                pe.wait_ge(lin_added, BANKS * (2 * v + g) + j + 1)
                t = g * BANKS + j
                for c in range(2):
                    rows = slice(0, ROWS[c] + c)
                    for part, gg in enumerate((g_h, g_l)):
                        ins = pe.matmul(bank[:, g, j, :], win[rows, k, c, t * P:(t + 1) * P],
                                        gg[rows, k, c, :], start=c == 0 and part == 0,
                                        stop=c == 1 and part == 1)
                ins.then_inc(conv_full, 1)

            def lift(q, g, j):
                pe.wait_ge(level_done, q + 1)
                pe.matmul(bank[:, g, j, :], level[:, g, :], shift_rows[:, j, :], start=False, stop=True,
                          skip_group_check=True
                          ).then_inc(shifted, 1)

            def step(b, f, k, first):
                v = b * TO + f
                for g in range(2):
                    was = before(f, g, first)
                    for j in range(3):
                        fill(v, k, g, j)
                    if was:
                        lift(2 * v + g - 1, was[1], 0)
                    fill(v, k, g, 3)
                    for j in range(1, BANKS):
                        if was:
                            lift(2 * v + g - 1, was[1], j)

            def flush(b):
                for j in range(BANKS):
                    lift(2 * (b * TO + TO) - 1, 1, j)

            batches(pe, step, flush)


def diagonal(w):
    n = w.shape[0]
    return w.rearrange("a b -> (a b)")[0:n * n:n + 1].rearrange("(k p) -> p k", p=P)


def build(nc, x, w_qkv, w_out, b_out, gn_gamma, gn_beta, w_mix, conv_w, conv_b, ln_gamma, ln_beta, out):
    def scratch(name, shape):
        return nc.dram_tensor(name, shape, F32, kind="Internal").ap()

    qk_hi = scratch("qk_hi", (2 * B * C, N))
    qk_lo = scratch("qk_lo", (2 * B * C, N))
    v_split = scratch("v_split", (G, P, NT, 2 * D))
    attended = scratch("attended", (G, N, D))
    x_mid = scratch("x_mid", (B * N, C))
    feat_rows = scratch("feat_rows", (B * N, C))
    chosen = scratch("chosen", (B * N, N))
    project_phase(nc, x, w_qkv, qk_hi, qk_lo, v_split)
    attention_phase(nc, qk_hi, qk_lo, v_split, attended)
    mixing_phase(nc, x, attended, w_out, b_out, gn_gamma, gn_beta, diagonal(w_mix), x_mid, feat_rows, chosen)
    convolution_phase(nc, chosen, feat_rows, x_mid, conv_w, conv_b, ln_gamma, ln_beta, out)


_INS = ["x", "L0_conv_w_qkv", "L0_conv_w_out", "L0_conv_b_out", "L0_conv_gamma", "L0_conv_beta", "L1_conv_W",
        "L1_conv_conv_w", "L1_conv_conv_b", "L1_conv_ln_gamma", "L1_conv_ln_beta"]


def kernel(**inputs):
    import numpy as np
    import concourse.bacc as bacc
    from concourse.bass_utils import run_bass_kernel_spmd

    nc = bacc.Bacc("TRN2", target_bir_lowering=False, num_devices=1)
    arrays, args = {}, []
    for name in _INS:
        a = np.ascontiguousarray(inputs[name])
        if name == "x":
            a = a.reshape(B * N, C)
        arrays["in_" + name] = a
        args.append(nc.dram_tensor("in_" + name, a.shape, mybir.dt.from_np(a.dtype), kind="ExternalInput").ap())
    out = nc.dram_tensor("out", (B * N, C), F32, kind="ExternalOutput").ap()
    build(nc, *args, out)
    r = run_bass_kernel_spmd(nc, [arrays], core_ids=[0])
    return r.results[0]["out"].reshape(8, 32, 32, 512)
```

```python
from contextlib import ExitStack

import concourse.bass as bass
from concourse import mybir

F32 = mybir.dt.float32
F32R = mybir.dt.float32r
BF16 = mybir.dt.bfloat16
ALU = mybir.AluOpType
ACT = mybir.ActivationFunctionType
AX = mybir.AxisListType

P = 128
B = 8
N = 1024
C = 512
NT = N // P
KC = C // P
HEADS = 8
D = C // HEADS
G = B * HEADS
HALF = 512
GROUP = 16
NG = C // GROUP
T = 32
M = 32
KS = 7
TO = T - KS + 1
GN_IN_EPS = 1e-5
GN_OUT_EPS = 1e-3
LN_EPS = 1e-5
SCALE = float(D) ** -0.5


class Chain:

    def __init__(self, engine, sem, start):
        self.engine, self.sem, self.start, self.n = engine, sem, start, 0

    def __call__(self, instruction):
        instruction.then_inc(self.sem, 1)
        self.n += 1
        self.engine.wait_ge(self.sem, self.start + self.n)


def project_phase(nc, x, w_qkv, qk_hi, qk_lo, v_split):
    QKT = 2 * C // P
    TILES = QKT * 2 + NT
    BANKS = 4
    SCHAIN = 5
    with ExitStack() as ctx:
        def sb(name, shape, dt):
            return ctx.enter_context(nc.sbuf_tensor("p1_" + name, shape, dt))

        def psum(name, shape, dt=F32):
            return ctx.enter_context(nc.psum_tensor("p1_" + name, shape, dt))

        def sem(name):
            return ctx.enter_context(nc.semaphore("p1_" + name))

        ident = sb("ident", [P, P], F32)
        gavg = sb("gavg", [P, P], F32)
        w_raw = sb("w_raw", [P, KC, 3 * C], F32)
        w_h = sb("w_h", [P, KC, 3 * C], F32R)
        w_l = sb("w_l", [P, KC, 3 * C], F32R)
        x_tok = sb("x_tok", [P, NT, C], F32)
        x_ch = sb("x_ch", [P, KC, N], F32)
        x_h = sb("x_h", [P, KC, N], F32R)
        x_l = sb("x_l", [P, KC, N], F32R)
        qk_out = sb("qk_out", [P, 2, 2, N], F32R)
        v_out = sb("v_out", [P, 2, HEADS, 2, D], F32R)
        bn = sb("bn", [P, KC, 2, 6], F32)
        mv = sb("mv", [P, KC, 2], F32)
        gm = sb("gm", [P, KC], F32)
        dev = sb("dev", [P, KC], F32)
        spread = sb("spread", [P, KC], F32)
        gvar = sb("gvar", [P, KC], F32)
        gstd = sb("gstd", [P, KC], F32)
        grstd = sb("grstd", [P, KC], F32)
        turned = psum("turned", [P, 2, HALF])
        stat = psum("stat", [P, HALF])
        prod = psum("prod", [P, BANKS, HALF])

        consts = sem("consts")
        w_loaded = sem("w_loaded")
        w_high = sem("w_high")
        w_low = sem("w_low")
        x_loaded = sem("x_loaded")
        turn_full = sem("turn_full")
        xch_ready = sem("xch_ready")
        mv_ready = sem("mv_ready")
        mean_ready = sem("mean_ready")
        dev_ready = sem("dev_ready")
        var_ready = sem("var_ready")
        std_in = sem("std_in")
        std_out = sem("std_out")
        normed = sem("normed")
        hi_x = sem("hi_x")
        lo_first = sem("lo_first")
        lo_second = sem("lo_second")
        prod_full = sem("prod_full")
        hi_done = sem("hi_done")
        lo_done = sem("lo_done")
        dchain = sem("dchain")
        qk_stored = [sem("qk_stored0"), sem("qk_stored1")]
        v_stored = [sem("v_stored0"), sem("v_stored1")]
        block = ctx.enter_context(nc.Block())

        def pipeline(engine, product, stage):
            for s in range(TILES):
                stage(s, 0, None)
            with engine.Fori(0, B - 1) as b:
                for q in range(TILES):
                    if q == TILES - 1:
                        stage(q, b + 1, b)
                        product(b, q)
                    else:
                        product(b, q)
                        stage(q, b + 1, b)
            for q in range(TILES):
                product(B - 1, q)

        def half(h):
            return slice(h * HALF, (h + 1) * HALF)

        TURN, STATS, MEAN, STD, NORM, SPLIT = 2, 10, 11, 12, 13, 2 * QKT + NT // 2

        @block.sync
        def _(sp):
            sp.dma_start(x_tok[:], x[0:N, :].rearrange("(t p) c -> p t c", p=P)).then_inc(x_loaded, 16)
            sp.dma_start(w_raw[:], w_qkv.rearrange("(k p) c -> p k c", p=P)).then_inc(w_loaded, 16)
            for k in range(2):
                sp.sem_inc(qk_stored[k], 16)
                sp.sem_inc(v_stored[k], 16)

            def load_x(b):
                sp.wait_ge(turn_full, b * 2 * KC)
                sp.dma_start(x_tok[:], x[bass.ds(b * N, N), :].rearrange("(t p) c -> p t c", p=P)
                             ).then_inc(x_loaded, 16)

            def stores(b, load):
                for m in range(QKT):
                    sp.wait_ge(lo_done, BANKS + b * TILES + 2 * m + 2)
                    row = m // (QKT // 2) * B * C + b * C + m % (QKT // 2) * P
                    sp.dma_start(qk_hi[bass.ds(row, P), :], qk_out[:, m % 2, 0, :].bitcast(F32)).then_inc(qk_stored[m % 2], 16)
                    sp.dma_start(qk_lo[bass.ds(row, P), :], qk_out[:, m % 2, 1, :].bitcast(F32)).then_inc(qk_stored[m % 2], 16)
                    if load and m == 5:
                        load_x(b + 2)
                for t in range(NT):
                    sp.wait_ge(lo_done, BANKS + b * TILES + 2 * QKT + t + 1)
                    sp.dma_start(v_split[bass.ds(b * HEADS, HEADS), :, t, :].rearrange("h p c -> p h c"),
                                 v_out[:, t % 2].rearrange("p h a d -> p h (a d)").bitcast(F32)).then_inc(v_stored[t % 2], 16)

            load_x(1)
            with sp.Fori(0, B - 2) as b:
                stores(b, True)
            stores(B - 2, False)
            stores(B - 1, False)
            for k in range(2):
                sp.wait_ge(qk_stored[k], 16 + B * QKT * 16)
                sp.wait_ge(v_stored[k], 16 + B * NT // 2 * 16)

        @block.gpsimd
        def _(pool):
            pool.memset(ident[:], 0.0).then_inc(consts, 1)
            pool.memset(gavg[:], 1.0 / GROUP).then_inc(consts, 1)
            pool.wait_ge(consts, 2)
            pool.affine_select(out=ident[:], in_=ident[:], compare_op=ALU.not_equal, fill=1.0, base=0,
                               pattern=[[-1, P]], channel_multiplier=1).then_inc(consts, 1)
            blocks = gavg[:].rearrange("p (g c) -> p g c", c=GROUP)
            pool.affine_select(out=blocks, in_=blocks, compare_op=ALU.is_ge, fill=0.0, base=0,
                               pattern=[[-GROUP, P // GROUP], [0, GROUP]], channel_multiplier=1).then_inc(consts, 1)
            pool.wait_ge(consts, 4)
            pool.affine_select(out=blocks, in_=blocks, compare_op=ALU.is_ge, fill=0.0, base=GROUP - 1,
                               pattern=[[GROUP, P // GROUP], [0, GROUP]], channel_multiplier=-1).then_inc(consts, 1)

            def stage(s, b, last):
                if s == SPLIT:
                    for k in range(KC):
                        pool.wait_ge(hi_x, b * 2 * KC + k + 1)
                        pool.tensor_tensor(x_l[:, k, half(0)], x_ch[:, k, half(0)],
                                           x_h[:, k, half(0)].bitcast(F32), ALU.subtract).then_inc(lo_first, 1)

            pipeline(pool, lambda b, q: None, stage)

        @block.scalar
        def _(act):
            act.sem_inc(xch_ready, 2)

            def product(b, q):
                if q < 2 * QKT:
                    m, j = q // 2, q % 2
                    if j == 0:
                        act.wait_ge(qk_stored[m % 2], 16 + b * QKT * 16 + m // 2 * 32)
                    act.wait_ge(prod_full, b * TILES + q + 1)
                    act.activation(qk_out[:, m % 2, 0, half(j)], prod[:, q % BANKS, :],
                                   ACT.Copy, scale=SCALE if m < QKT // 2 else 1.0).then_inc(hi_done, 1)
                else:
                    t = q - 2 * QKT
                    act.wait_ge(v_stored[t % 2], 16 + b * NT // 2 * 16 + t // 2 * 16)
                    act.wait_ge(prod_full, b * TILES + q + 1)
                    act.activation(v_out[:, t % 2, :, 0, :],
                                   prod[:, q % BANKS, :].rearrange("p (h d) -> p h d", d=D),
                                   ACT.Copy).then_inc(hi_done, 1)

            def stage(s, b, last):
                if TURN <= s < TURN + 2 * KC:
                    g = s - TURN
                    act.wait_ge(turn_full, b * 2 * KC + g + 1)
                    act.activation(x_ch[:, g // 2, half(g % 2)], turned[:, g % 2, :], ACT.Copy).then_inc(xch_ready, 1)
                if s == STD:
                    act.wait_ge(std_in, b + 1)
                    act.activation(gstd[:], gvar[:], ACT.Sqrt).then_inc(std_out, 1)
                if s == NORM and last is None:
                    act.wait_ge(w_loaded, 16)
                    for k in range(KC):
                        act.activation(w_h[:, k, :], w_raw[:, k, :], ACT.Copy).then_inc(w_high, 1)
                if s in (SPLIT, TILES - 1):
                    h = int(s != SPLIT)
                    if last is not None:
                        act.wait_ge(prod_full, last * TILES + (TILES if h else SPLIT))
                    for k in range(KC):
                        act.wait_ge(normed, b * KC + k + 1)
                        act.activation(x_h[:, k, half(h)], x_ch[:, k, half(h)], ACT.Copy).then_inc(hi_x, 1)

            pipeline(act, product, stage)

        @block.vector
        def _(dve):
            dve.sem_inc(lo_done, BANKS)

            def product(b, q):
                dve.wait_ge(hi_done, b * TILES + q + 1)
                if q < 2 * QKT:
                    m, j = q // 2, q % 2
                    dve.scalar_tensor_tensor(qk_out[:, m % 2, 1, half(j)], prod[:, q % BANKS, :],
                                             SCALE if m < QKT // 2 else 1.0, qk_out[:, m % 2, 0, half(j)].bitcast(F32),
                                             ALU.mult, ALU.subtract).then_inc(lo_done, 1)
                else:
                    t = q - 2 * QKT
                    dve.tensor_tensor(v_out[:, t % 2, :, 1, :],
                                      prod[:, q % BANKS, :].rearrange("p (h d) -> p h d", d=D),
                                      v_out[:, t % 2, :, 0, :].bitcast(F32), ALU.subtract).then_inc(lo_done, 1)

            def stage(s, b, last):
                link = Chain(dve, dchain, b * SCHAIN + (1 if s == MEAN else 4 if s == NORM else 0))
                if TURN <= s < TURN + 2 * KC:
                    g = s - TURN
                    dve.wait_ge(xch_ready, 2 + b * 2 * KC + g + 1)
                    ins = dve.bn_stats(bn[:, g // 2, g % 2, :], x_ch[:, g // 2, half(g % 2)])
                    if g == 2 * KC - 1:
                        link(ins)
                if s == STATS:
                    dve.memset(dev[:], 0.0)
                    for k in range(KC):
                        ins = dve.bn_aggr(mv[:, k, :], bn[:, k, :, :].rearrange("p a s -> p (a s)"))
                    ins.then_inc(mv_ready, 1)
                if s == MEAN:
                    dve.wait_ge(mean_ready, b + 1)
                    link(dve.tensor_copy(gm[:], stat[:, 0:KC]))
                    link(dve.tensor_tensor(dev[:], mv[:, :, 0], gm[:], ALU.subtract))
                    link(dve.tensor_tensor(dev[:], dev[:], dev[:], ALU.mult))
                    dve.tensor_tensor(spread[:], dev[:], mv[:, :, 1], ALU.add).then_inc(dev_ready, 1)
                if s == STD:
                    dve.wait_ge(var_ready, b + 1)
                    dve.tensor_scalar(gvar[:], stat[:, KC:2 * KC], GN_IN_EPS, None, ALU.add).then_inc(std_in, 1)
                if s == NORM:
                    dve.wait_ge(std_out, b + 1)
                    link(dve.reciprocal(grstd[:], gstd[:]))
                if NORM <= s < NORM + KC:
                    k = s - NORM
                    dve.tensor_scalar(x_ch[:, k, :], x_ch[:, k, :], gm[:, k:k + 1], grstd[:, k:k + 1],
                                      ALU.subtract, ALU.mult).then_inc(normed, 1)
                if s == NORM + KC and last is None:
                    for k in range(KC):
                        dve.wait_ge(w_high, k + 1)
                        dve.tensor_tensor(w_l[:, k, :], w_raw[:, k, :], w_h[:, k, :].bitcast(F32),
                                          ALU.subtract).then_inc(w_low, 1)
                if s == TILES - 1:
                    for k in range(KC):
                        dve.wait_ge(hi_x, b * 2 * KC + KC + k + 1)
                        dve.tensor_tensor(x_l[:, k, half(1)], x_ch[:, k, half(1)],
                                          x_h[:, k, half(1)].bitcast(F32), ALU.subtract).then_inc(lo_second, 1)

            pipeline(dve, product, stage)

        @block.tensor
        def _(pe):
            pe.wait_ge(consts, 5)

            def product(b, q):
                bank = prod[:, q % BANKS, :]
                if q == 0:
                    pe.wait_ge(w_low, KC)
                    pe.wait_ge(lo_first, b * KC + KC)
                if q == 1:
                    pe.wait_ge(lo_second, b * KC + KC)
                pe.wait_ge(lo_done, b * TILES + q + 1)
                for n, (w, xx) in enumerate(((w_h, x_h), (w_h, x_l), (w_l, x_h))):
                    for k in range(KC):
                        flags = dict(start=(n == 0 and k == 0), stop=(n == 2 and k == KC - 1))
                        if q < 2 * QKT:
                            m, j = q // 2, q % 2
                            ins = pe.matmul(bank, w[:, k, m * P:(m + 1) * P], xx[:, k, half(j)], **flags)
                        else:
                            t = q - 2 * QKT
                            ins = pe.matmul(bank, xx[:, k, t * P:(t + 1) * P], w[:, k, 2 * C:3 * C], **flags)
                ins.then_inc(prod_full, 1)

            def stage(s, b, last):
                if TURN <= s < TURN + 2 * KC:
                    g = s - TURN
                    if g == 0:
                        pe.wait_ge(x_loaded, b * 16 + 16)
                    pe.wait_ge(xch_ready, b * 2 * KC + g + 1)
                    for j in range(4):
                        t = g % 2 * 4 + j
                        ins = pe.transpose(turned[:, g % 2, j * P:(j + 1) * P],
                                           x_tok[:, t, g // 2 * P:(g // 2 + 1) * P], ident[:])
                    ins.then_inc(turn_full, 1)
                if s == MEAN:
                    pe.wait_ge(mv_ready, b + 1)
                    pe.matmul(stat[:, 0:KC], gavg[:], mv[:, :, 0], start=True, stop=True).then_inc(mean_ready, 1)
                if s == STD:
                    pe.wait_ge(dev_ready, b + 1)
                    pe.matmul(stat[:, KC:2 * KC], gavg[:], spread[:], start=True, stop=True).then_inc(var_ready, 1)

            pipeline(pe, product, stage)


def attention_phase(nc, qk_hi, qk_lo, v_split, attended):
    STEPS = NT
    QUARTERS = 4
    with ExitStack() as ctx:
        def sb(name, shape, dt):
            return ctx.enter_context(nc.sbuf_tensor("p2_" + name, shape, dt))

        def psum(name, shape, dt=F32):
            return ctx.enter_context(nc.psum_tensor("p2_" + name, shape, dt))

        def sem(name):
            return ctx.enter_context(nc.semaphore("p2_" + name))

        ident = sb("ident", [P, P], F32)
        twice = sb("twice", [P, D], F32)
        k_st = sb("k_st", [P, 2, N], F32R)
        q_hh = sb("q_hh", [P, 2, N], F32R)
        q_l0 = sb("q_l0", [P, 2, N], F32R)
        v_st = sb("v_st", [P, 2, NT, 2 * D], F32R)
        expd = sb("expd", [P, 2, N], F32)
        e_h = sb("e_h", [P, 2, NT, HALF], F32R)
        e_l = sb("e_l", [P, 2, NT, HALF], F32R)
        o_sb = sb("o_sb", [P, 2, HALF], F32)
        res = sb("res", [P, 2, 4, D], F32)
        nmax = sb("nmax", [P, STEPS], F32)
        rows = sb("rows", [P, 2, STEPS], F32)
        rinv = sb("rinv", [P, 2, 4], F32)
        score = psum("score", [P, 2, N])
        turned = psum("turned", [P, 2, HALF])
        out_ps = psum("out_ps", [P, HALF])
        row_ps = psum("row_ps", [P, HALF])

        consts = sem("consts")
        zeroed = sem("zeroed")
        kq_loaded = [sem("kq_loaded0"), sem("kq_loaded1")]
        v_loaded = [sem("v_loaded0"), sem("v_loaded1")]
        scored = sem("scored")
        maxed = sem("maxed")
        exped = sem("exped")
        turn_full = sem("turn_full")
        hi_done = sem("hi_done")
        lo_done = sem("lo_done")
        av_done = sem("av_done")
        o_copied = sem("o_copied")
        rows_full = sem("rows_full")
        rinv_done = sem("rinv_done")
        res_done = sem("res_done")
        stored = [sem("stored0"), sem("stored1")]
        def in_pairs(engine, pair):
            pair(0, True, False)
            with engine.Fori(2, G - 2, 2) as g:
                pair(g, False, False)
            pair(G - 2, False, True)

        block = ctx.enter_context(nc.Block())

        @block.gpsimd
        def _(pool):
            pool.memset(ident[:], 0.0).then_inc(consts, 1)
            pool.memset(twice[:], 0.0).then_inc(consts, 1)
            pool.wait_ge(consts, 2)
            pool.affine_select(out=ident[:], in_=ident[:], compare_op=ALU.not_equal, fill=1.0, base=0,
                               pattern=[[-1, P]], channel_multiplier=1).then_inc(consts, 1)
            pool.affine_select(out=twice[:], in_=twice[:], compare_op=ALU.not_equal, fill=1.0, base=0,
                               pattern=[[-1, D]], channel_multiplier=1).then_inc(consts, 1)
            pool.wait_ge(consts, 4)
            pool.affine_select(out=twice[:], in_=twice[:], compare_op=ALU.not_equal, fill=1.0, base=-D,
                               pattern=[[-1, D]], channel_multiplier=1).then_inc(consts, 1)

        @block.sync
        def _(sp):
            def load(g, k):
                q_row, k_row = g * D, B * C + g * D
                for at, row, dst, src in ((0, k_row, k_st, qk_hi), (D, k_row, k_st, qk_lo),
                                          (0, q_row, q_hh, qk_hi), (D, q_row, q_hh, qk_hi),
                                          (0, q_row, q_l0, qk_lo)):
                    sp.dma_start(dst[at:at + D, k, :].bitcast(F32), src[bass.ds(row, D), :]).then_inc(kq_loaded[k], 16)

            def load_v(g, k):
                sp.dma_start(v_st[:, k].bitcast(F32), v_split[bass.ds(g, 1)].rearrange("o p t c -> p (o t) c")
                             ).then_inc(v_loaded[k], 16)

            def store(g, h, k):
                sp.wait_ge(res_done, 1 + 2 * g + h + 1)
                sp.dma_start(attended[bass.ds(g, 1), h * HALF:(h + 1) * HALF, :].rearrange("o (t p) d -> p (o t) d", p=P),
                             res[:, h]).then_inc(stored[h], 16)

            def pair(g, first=False, last=False):
                for k in range(2):
                    if not (last and k == 1):
                        if not (first and k == 0):
                            sp.wait_ge(scored, STEPS * (g + k))
                        load(g + k + 1, (k + 1) % 2)
                        if not (first and k == 0):
                            sp.wait_ge(av_done, 2 * (g + k))
                        load_v(g + k + 1, (k + 1) % 2)
                    if not (first and k == 0):
                        store(g + k - 1, 1, (k + 1) % 2)
                    store(g + k, 0, k)

            sp.sem_inc(stored[0], 16)
            sp.sem_inc(stored[1], 16)
            load(0, 0)
            load_v(0, 0)
            in_pairs(sp, pair)
            store(G - 1, 1, 1)
            for h in range(2):
                sp.wait_ge(stored[h], 16 + 16 * G)

        @block.tensor
        def _(pe):
            def scores(g, k, s):
                n = g * STEPS + s
                if s == 0:
                    pe.wait_ge(kq_loaded[k], 80 * (g // 2 + 1) if isinstance(g, int) else (g + 2 - k) * 40)
                if not (isinstance(n, int) and n < 2):
                    pe.wait_ge(exped, n - 1)
                for j in range(2):
                    for part, q in enumerate((q_hh, q_l0)):
                        ins = pe.matmul(score[:, s % 2, j * HALF:(j + 1) * HALF], q[:, k, s * P:(s + 1) * P],
                                        k_st[:, k, j * HALF:(j + 1) * HALF], start=part == 0, stop=part == 1)
                ins.then_inc(scored, 1)

            def turn(g, k, s):
                n = g * STEPS + s
                pe.wait_ge(exped, n + 1)
                for j in range(2):
                    pe.wait_ge(lo_done, 2 * n + j + 1)
                    for i in range(4):
                        t = 4 * j + i
                        ins = pe.transpose(turned[:, j, i * P:(i + 1) * P], expd[:, s % 2, t * P:(t + 1) * P], ident[:])
                    ins.then_inc(turn_full, 1)

            def av(g, k, h, r):
                n = 2 * g + h
                if r == 0:
                    pe.wait_ge(lo_done, 2 + 8 * n + 8)
                    pe.wait_ge(o_copied, n + 1)
                    if h == 0:
                        pe.wait_ge(v_loaded[k], 16 * (g // 2 + 1) if isinstance(g, int) else (g + 2 - k) * 8)
                for t in (2 * r, 2 * r + 1):
                    for part, e in enumerate((e_h, e_l)):
                        ins = pe.matmul(out_ps[:], v_st[:, k, t, :], e[:, h, t, :],
                                        start=t == 0 and part == 0, stop=t == NT - 1 and part == 1)
                if r == QUARTERS - 1:
                    ins.then_inc(av_done, 1)

            def to_rows(g, h):
                n = 2 * g + h
                pe.wait_ge(o_copied, 1 + n + 1)
                pe.wait_ge(res_done, n + 1)
                for i in range(4):
                    ins = pe.matmul(row_ps[:, i * D:(i + 1) * D], o_sb[:, h, i * P:(i + 1) * P], twice[:],
                                    start=True, stop=True)
                ins.then_inc(rows_full, 1)

            def pair(g0, first, last):
                for k in range(2):
                    g = g0 + k
                    for s in range(STEPS):
                        if s < STEPS - 2:
                            scores(g, k, s + 2)
                        elif not (last and k == 1):
                            scores(g + 1, 1 - k, s + 2 - STEPS)
                        turn(g, k, s)
                        early = first and k == 0
                        if s < 4:
                            if not early:
                                av(g - 1, 1 - k, 1, s)
                        else:
                            av(g, k, 0, s - 4)
                        if s == 0 and not early:
                            to_rows(g - 1, 0)
                        if s == 4 and not early:
                            to_rows(g - 1, 1)

            pe.wait_ge(consts, 5)
            pe.wait_ge(zeroed, 1)
            scores(0, 0, 0)
            scores(0, 0, 1)
            in_pairs(pe, pair)
            for r in range(QUARTERS):
                av(G - 1, 1, 1, r)
            to_rows(G - 1, 0)
            to_rows(G - 1, 1)

        @block.scalar
        def _(act):
            def exp(g, k, s):
                n = g * STEPS + s
                act.wait_ge(maxed, n + 1)
                if not (isinstance(n, int) and n < 2):
                    act.wait_ge(turn_full, 2 * (n - 1))
                act.activation(expd[:, s % 2, :], score[:, s % 2, :], ACT.Exp, bias=nmax[:, s:s + 1],
                               accum_out=rows[:, k, s:s + 1]).then_inc(exped, 1)

            def high(g, s):
                n = g * STEPS + s
                for j in range(2):
                    act.wait_ge(turn_full, 2 * n + j + 1)
                    if s % 4 == 0 and not (isinstance(g, int) and g == 0):
                        act.wait_ge(av_done, 2 * g - 2 + s // 4 + 1)
                    act.activation(e_h[:, s // 4, 4 * j:4 * j + 4, s % 4 * P:(s % 4 + 1) * P],
                                   turned[:, j, :].rearrange("p (t i) -> p t i", i=P), ACT.Copy).then_inc(hi_done, 1)

            def copy_out(g, h):
                n = 2 * g + h
                act.wait_ge(av_done, n + 1)
                act.activation(o_sb[:, h, :], out_ps[:], ACT.Copy).then_inc(o_copied, 1)

            def pair(g0, first, last):
                for k in range(2):
                    g = g0 + k
                    for s in range(STEPS):
                        if s == 0 and not (first and k == 0):
                            copy_out(g - 1, 0)
                        if s == 4 and not (first and k == 0):
                            copy_out(g - 1, 1)
                        if s < STEPS - 1:
                            exp(g, k, s + 1)
                        elif not (last and k == 1):
                            exp(g + 1, 1 - k, 0)
                        high(g, s)

            act.sem_inc(o_copied, 1)
            exp(0, 0, 0)
            in_pairs(act, pair)
            copy_out(G - 1, 0)
            copy_out(G - 1, 1)

        @block.vector
        def _(dve):
            def maximum(g, s):
                n = g * STEPS + s
                dve.wait_ge(scored, n + 1)
                dve.tensor_reduce(nmax[:, s:s + 1], score[:, s % 2, :], AX.X, ALU.max, negate=True).then_inc(maxed, 1)

            def low(g, s):
                n = g * STEPS + s
                for j in range(2):
                    dve.wait_ge(hi_done, 2 * n + j + 1)
                    part = [x[:, s // 4, 4 * j:4 * j + 4, s % 4 * P:(s % 4 + 1) * P] for x in (e_h, e_l)]
                    dve.tensor_tensor(part[1], turned[:, j, :].rearrange("p (t i) -> p t i", i=P),
                                      part[0].bitcast(F32), ALU.subtract).then_inc(lo_done, 1)

            def finish(g, k, h):
                n = 2 * g + h
                dve.wait_ge(rows_full, n + 1)
                dve.reciprocal(rinv[:, h, :], rows[:, k, 4 * h:4 * h + 4]).then_inc(rinv_done, 1)
                dve.wait_ge(rinv_done, n + 1)
                dve.wait_ge(stored[h], 16 + 16 * g)
                dve.tensor_tensor(res[:, h], row_ps[:, 0:4 * D].rearrange("p (t d) -> p t d", d=D),
                                  rinv[:, h, :].unsqueeze(2).to_broadcast([P, 4, D]), ALU.mult).then_inc(res_done, 1)

            def pair(g0, first, last):
                for k in range(2):
                    g = g0 + k
                    for s in range(STEPS):
                        if s < STEPS - 2:
                            maximum(g, s + 2)
                        elif not (last and k == 1):
                            maximum(g + 1, s + 2 - STEPS)
                        low(g, s)
                        if s == 0 and not (first and k == 0):
                            finish(g - 1, 1 - k, 0)
                        if s == 4 and not (first and k == 0):
                            finish(g - 1, 1 - k, 1)

            dve.memset(q_l0[D:P, :, :].bitcast(F32), 0.0).then_inc(zeroed, 1)
            dve.sem_inc(lo_done, 2)
            dve.sem_inc(res_done, 1)
            maximum(0, 0)
            maximum(0, 1)
            in_pairs(dve, pair)
            finish(G - 1, 1, 0)
            finish(G - 1, 1, 1)


def mixing_phase(nc, x, attended, w_out, b_out, gamma, beta, w_diag, x_mid, feat_rows, chosen):
    BANKS = 4
    DCHAIN = 7
    LINKS = (0, 0, 0, 1, 3, 4, 4, 5)
    with ExitStack() as ctx:
        def sb(name, shape, dt=F32):
            return ctx.enter_context(nc.sbuf_tensor("p3_" + name, shape, dt))

        def psum(name, shape, dt=F32):
            return ctx.enter_context(nc.psum_tensor("p3_" + name, shape, dt))

        def sem(name):
            return ctx.enter_context(nc.semaphore("p3_" + name))

        ident = sb("ident", [P, P])
        ident_b = sb("ident_b", [P, P], BF16)
        all_avg = sb("all_avg", [P, P])
        grp_avg = sb("grp_avg", [P, P])
        ramp = sb("ramp", [P, M], BF16)
        w_h = sb("w_h", [P, KC, C], F32R)
        w_l = sb("w_l", [P, KC, C], F32R)
        bias = sb("bias", [P, C])
        gam = sb("gam", [P, C])
        bet = sb("bet", [P, C])
        gam_r = sb("gam_r", [P, C])
        diag = sb("diag", [P, KC])
        o_h = sb("o_h", [P, KC, N], F32R)
        o_l = sb("o_l", [P, KC, N], F32R)
        x_tok = sb("x_tok", [P, NT, C])
        y = sb("y", [P, NT, C])
        work = sb("work", [P, NT, C])
        n_h = sb("n_h", [P, KC, N], F32R)
        n_l = sb("n_l", [P, KC, N], F32R)
        m_h = sb("m_h", [P, KC, N], F32R)
        m_l = sb("m_l", [P, KC, N], F32R)
        w_raw = work[:, 0:KC, :]
        ysum = sb("ysum", [P, NT])
        ysq = sb("ysq", [P, NT])
        col = sb("col", [P, 8])
        gmean = sb("gmean", [P, NG])
        gvar = sb("gvar", [P, NG])
        gstd = sb("gstd", [P, NG])
        grstd = sb("grstd", [P, NG])
        nsq = sb("nsq", [P, NT])
        nstd = sb("nstd", [P, NT])
        nrec = sb("nrec", [P, NT])
        top = sb("top", [P, 2, T])
        equal = sb("equal", [P, 2, N], BF16)
        ranked = sb("ranked", [P, 2, N], BF16)
        best = sb("best", [P, 2, T], BF16)
        onehot = sb("onehot", [P, 2, N], BF16)
        oh_out = sb("oh_out", [P, 2, NT, P], F32R)
        total, mean_c, sq_c, var_c, std_c, rstd_c, neg_c = (col[:, i:i + 1] for i in range(7))

        prod = psum("prod", [P, 2, 2, HALF])
        turned = prod[:].rearrange("p a h n -> p (a h) n")
        proj = psum("proj", [P, 2, HALF])
        stat = psum("stat", [P, HALF])
        oh_ps = psum("oh_ps", [P, NT, P], BF16)

        consts = sem("consts")
        c_loaded = sem("c_loaded")
        w_high = sem("w_high")
        w_low = sem("w_low")
        o_loaded = sem("o_loaded")
        x_loaded = sem("x_loaded")
        o_high = sem("o_high")
        o_low = sem("o_low")
        x_beta = sem("x_beta")
        prod_full = sem("prod_full")
        y_done = sem("y_done")
        totals = sem("totals")
        averaged = sem("averaged")
        centre = sem("centre")
        squared = sem("squared")
        std_in = sem("std_in")
        std_out = sem("std_out")
        y_scaled = sem("y_scaled")
        mid_low = sem("mid_low")
        mid_high = sem("mid_high")
        colsum = sem("colsum")
        centred = sem("centred")
        dev_sq = sem("dev_sq")
        grstd_done = sem("grstd_done")
        feat_even = sem("feat_even")
        feat_odd = sem("feat_odd")
        norm_sq = sem("norm_sq")
        unit = sem("unit")
        turn_full = sem("turn_full")
        high_done = sem("high_done")
        low_done = sem("low_done")
        sim_full = sem("sim_full")
        eq_done = sem("eq_done")
        rank_done = sem("rank_done")
        best_top = sem("best_top")
        best_done = sem("best_done")
        hot_done = sem("hot_done")
        hot_turned = sem("hot_turned")
        hot_out = sem("hot_out")
        dchain = sem("dchain")
        mid_stored = sem("mid_stored")
        feat_stored = sem("feat_stored")
        hot_stored = [sem("hot_stored0"), sem("hot_stored1")]
        block = ctx.enter_context(nc.Block())

        def per_group(v):
            return v.unsqueeze(2).to_broadcast([P, NG, GROUP])

        def pipeline(engine, similar, stage, turn, hot=None):
            for s in range(NT):
                stage(s, 0)
            turn(0, False)
            with engine.Fori(0, B - 1) as b:
                for t in range(NT):
                    similar(b, t)
                    stage(t, b + 1)
                    if hot and t > 0:
                        hot(b, t - 1)
                turn(b + 1, True)
            for t in range(NT):
                similar(B - 1, t)
                if hot and t > 0:
                    hot(B - 1, t - 1)

        @block.sync
        def _(sp):
            att = attended.rearrange("g i d -> (g i d)").rearrange("(r n) -> r n", n=N)
            load_o = lambda b: sp.dma_start(o_l[:].bitcast(F32), att[bass.ds(b * C, C), :].rearrange(
                "(k p) n -> p k n", p=P)).then_inc(o_loaded, 16)
            load_x = lambda b: sp.dma_start(x_tok[:], x[bass.ds(b * N, N), :].rearrange("(t p) c -> p t c", p=P)
                                            ).then_inc(x_loaded, 16)
            load_o(0)
            sp.dma_start(w_raw, w_out.rearrange("(k p) c -> p k c", p=P)).then_inc(c_loaded, 16)
            for row, src in ((bias, b_out), (gam, gamma), (bet, beta)):
                sp.dma_start(row[:], src.partition_broadcast(P)).then_inc(c_loaded, 16)
            with nc.allow_non_contiguous_dma("512 numbers of a diagonal, once"):
                sp.dma_start(diag[:], w_diag).then_inc(c_loaded, 16)
            load_x(0)
            sp.sem_inc(feat_stored, 16)
            for h in hot_stored:
                sp.sem_inc(h, 16)

            def hot(b, t):
                sp.wait_ge(hot_out, 1 + b * NT + t + 1)
                sp.dma_start(chosen[bass.ds(b * N, N), t * P:(t + 1) * P].rearrange("(j p) n -> p j n", p=P),
                             oh_out[:, t % 2].bitcast(F32)).then_inc(hot_stored[t % 2], 16)

            def stage(s, b, last=False):
                if s == 2:
                    sp.wait_ge(prod_full, b * NT + NT)
                    load_o(0 if last else b + 1)
                if s == 4:
                    sp.wait_ge(mid_low, b + 1)
                    sp.wait_ge(mid_high, b + 1)
                    sp.dma_start(x_mid[bass.ds(b * N, N), :].rearrange("(t p) c -> p t c", p=P), x_tok[:]
                                 ).then_inc(mid_stored, 16)
                if s == 5 and not last:
                    sp.wait_ge(mid_stored, b * 16 + 16)
                    sp.wait_ge(centred, b * NT + NT)
                    load_x(b + 1)
                if s == 7:
                    sp.wait_ge(feat_even, b * (NT // 2) + NT // 2)
                    sp.wait_ge(feat_odd, b * (NT // 2) + NT // 2)
                    sp.dma_start(feat_rows[bass.ds(b * N, N), :].rearrange("(t p) c -> p t c", p=P), y[:]
                                 ).then_inc(feat_stored, 16)

            def both(b, last):
                for t in range(NT):
                    stage(t, b + 1, last)
                    if t > 0:
                        hot(b, t - 1)
                hot(b, NT - 1)

            for s in range(NT):
                stage(s, 0)
            with sp.Fori(0, B - 2) as b:
                both(b, False)
            both(B - 2, True)
            for t in range(NT):
                hot(B - 1, t)
            sp.wait_ge(o_loaded, 16 * B + 16)
            sp.wait_ge(mid_stored, 16 * B)
            sp.wait_ge(feat_stored, 16 + 16 * B)
            for h in hot_stored:
                sp.wait_ge(h, 16 + 16 * B * NT // 2)

        @block.gpsimd
        def _(pool):
            n = 0
            for ins in (lambda: pool.memset(ident[:], 0.0),
                        lambda: pool.memset(all_avg[:], 1.0 / (N * C)),
                        lambda: pool.memset(grp_avg[:], 1.0 / (N * GROUP)),
                        lambda: pool.affine_select(out=ident[:], in_=ident[:], compare_op=ALU.not_equal, fill=1.0,
                                                   base=0, pattern=[[-1, P]], channel_multiplier=1),
                        lambda: pool.tensor_copy(ident_b[:], ident[:]),
                        lambda: pool.iota(ramp[:], pattern=[[-1, M]], base=M, channel_multiplier=0,
                                          allow_small_or_imprecise_dtypes=True)):
                ins().then_inc(consts, 1)
                n += 1
                pool.wait_ge(consts, n)
            ranks = ramp[:].unsqueeze(1).to_broadcast([P, T, M])

            def low_part(b, k):
                pool.wait_ge(o_high, b * KC + k + 1)
                pool.tensor_tensor(o_l[:, k, :], o_l[:, k, :].bitcast(F32), o_h[:, k, :].bitcast(F32),
                                   ALU.subtract).then_inc(o_low, 1)

            def stage(s, b):
                if s < 2:
                    pool.wait_ge(x_loaded, b * 16 + 16)
                    tiles = slice(s * NT // 2, (s + 1) * NT // 2)
                    pool.tensor_tensor(x_tok[:, tiles, :], x_tok[:, tiles, :],
                                       bet[:].unsqueeze(1).to_broadcast([P, NT // 2, C]), ALU.add
                                       ).then_inc(x_beta, 1)
                if s == 3:
                    pool.wait_ge(y_scaled, 2 * b + 1)
                    pool.wait_ge(x_beta, 2 * b + 1)
                    pool.tensor_tensor(x_tok[:, 0:NT // 2, :], x_tok[:, 0:NT // 2, :], y[:, 0:NT // 2, :], ALU.add
                                       ).then_inc(mid_low, 1)
                if s == 6:
                    pool.wait_ge(grstd_done, b + 1)
                    for t in range(1, NT, 2):
                        tile = y[:, t, :].rearrange("p (g c) -> p g c", c=GROUP)
                        pool.tensor_tensor(tile, tile, per_group(grstd[:]), ALU.mult).then_inc(feat_odd, 1)
                if s in (2, 4, 5, 7):
                    low_part(b + 1, (2, 4, 5, 7).index(s))

            def similar(b, t):
                pool.wait_ge(eq_done, b * NT + t + 1)
                if t >= 2:
                    pool.wait_ge(hot_done, b * NT + t - 1)
                pool.tensor_tensor(ranked[:, t % 2, :].rearrange("p (t m) -> p t m", m=M),
                                   equal[:, t % 2, :].rearrange("p (t m) -> p t m", m=M),
                                   ranks, ALU.mult).then_inc(rank_done, 1)

            for k in range(KC):
                low_part(0, k)
            pool.wait_ge(c_loaded, 16 * 5)
            pipeline(pool, similar, stage, lambda b, inside: None)

        @block.scalar
        def _(act):
            act.sem_inc(hot_out, 1)

            def high_part(b, k):
                act.wait_ge(o_loaded, b * 16 + 16)
                act.activation(o_h[:, k, :], o_l[:, k, :].bitcast(F32), ACT.Copy).then_inc(o_high, 1)

            def hot(b, t):
                act.wait_ge(hot_stored[t % 2], 16 + b * 16 * (NT // 2) + t // 2 * 16)
                act.wait_ge(hot_turned, b * NT + t + 1)
                act.activation(oh_out[:, t % 2], oh_ps[:], ACT.Copy).then_inc(hot_out, 1)

            def stage(s, b):
                if s == 2:
                    act.wait_ge(centre, b + 1)
                    for t in range(NT):
                        act.activation(work[:, t, :], y[:, t, :], ACT.Square, bias=neg_c,
                                       accum_out=ysq[:, t:t + 1]).then_inc(squared, 1)
                if s == 3:
                    act.wait_ge(std_in, b * 2 + 1)
                    act.activation(std_c, var_c, ACT.Sqrt).then_inc(std_out, 1)
                if s == 4:
                    for t in range(NT):
                        act.wait_ge(centred, b * NT + t + 1)
                        act.activation(work[:, t, :], y[:, t, :], ACT.Square).then_inc(dev_sq, 1)
                if s == 6:
                    act.wait_ge(std_in, b * 2 + 2)
                    act.activation(gstd[:], gvar[:], ACT.Sqrt).then_inc(std_out, 1)
                    for t in range(NT):
                        act.wait_ge((feat_even, feat_odd)[t % 2], b * (NT // 2) + t // 2 + 1)
                        act.activation(work[:, t, :], y[:, t, :], ACT.Square,
                                       accum_out=nsq[:, t:t + 1]).then_inc(norm_sq, 1)
                if s == 7:
                    act.wait_ge(norm_sq, b * NT + NT)
                    act.activation(nstd[:], nsq[:], ACT.Sqrt).then_inc(std_out, 1)
                if s in (2, 3, 4, 6):
                    high_part(b + 1, (2, 3, 4, 6).index(s))

            def turn(b, inside):
                if inside:
                    hot(b - 1, NT - 1)
                for g in range(2 * KC):
                    cols = slice(g % 2 * HALF, (g % 2 + 1) * HALF)
                    act.wait_ge(turn_full, b * 2 * KC + g + 1)
                    act.activation(n_h[:, g // 2, cols], turned[:, g % BANKS, :], ACT.Copy).then_inc(high_done, 1)
                    act.activation(m_h[:, g // 2, cols], turned[:, g % BANKS, :], ACT.Copy,
                                   scale=diag[:, g // 2:g // 2 + 1]).then_inc(high_done, 1)

            for k in range(KC):
                high_part(0, k)
            act.wait_ge(c_loaded, 16 * 5)
            for k in range(KC):
                act.activation(w_h[:, k, :], w_raw[:, k, :], ACT.Copy).then_inc(w_high, 1)
            pipeline(act, lambda b, t: None, stage, turn, hot)
            hot(B - 1, NT - 1)

        @block.vector
        def _(dve):
            for k in range(KC):
                dve.wait_ge(w_high, k + 1)
                dve.tensor_tensor(w_l[:, k, :], w_raw[:, k, :], w_h[:, k, :].bitcast(F32),
                                  ALU.subtract).then_inc(w_low, 1)

            def stage(s, b):
                link = Chain(dve, dchain, b * DCHAIN + LINKS[s])
                if s < 2:
                    if s == 0:
                        dve.wait_ge(feat_stored, 16 + b * 16)
                    for t in (range(5), range(5, NT))[s]:
                        dve.wait_ge(prod_full, b * NT + t + 1)
                        dve.scalar_tensor_tensor(y[:, t, :], proj[:, t % 2, :], 1.0, bias[:], ALU.mult, ALU.add,
                                                 accum_out=ysum[:, t:t + 1]).then_inc(y_done, 1)
                if s == 1:
                    dve.wait_ge(y_done, b * NT + NT)
                    dve.tensor_reduce(total, ysum[:], AX.X, ALU.add).then_inc(totals, 1)
                if s == 2:
                    dve.wait_ge(averaged, b * 2 + 1)
                    link(dve.tensor_copy(mean_c, stat[:, 0:1]))
                    dve.tensor_scalar(neg_c, mean_c, -1.0, None, ALU.mult).then_inc(centre, 1)
                if s == 3:
                    dve.wait_ge(squared, b * NT + NT)
                    dve.tensor_reduce(sq_c, ysq[:], AX.X, ALU.add).then_inc(totals, 1)
                    dve.wait_ge(averaged, b * 2 + 2)
                    dve.tensor_scalar(var_c, stat[:, 1:2], GN_OUT_EPS, None, ALU.add).then_inc(std_in, 1)
                    dve.wait_ge(std_out, b * 3 + 1)
                    link(dve.reciprocal(rstd_c, std_c))
                    link(dve.tensor_scalar(gam_r[:], gam[:], rstd_c, None, ALU.mult))
                    for h in range(2):
                        tiles = slice(h * NT // 2, (h + 1) * NT // 2)
                        dve.scalar_tensor_tensor(y[:, tiles, :], y[:, tiles, :], mean_c,
                                                 gam_r[:].unsqueeze(1).to_broadcast([P, NT // 2, C]),
                                                 ALU.subtract, ALU.mult).then_inc(y_scaled, 1)
                    dve.wait_ge(y_scaled, 2 * b + 2)
                    dve.wait_ge(x_beta, 2 * b + 2)
                    dve.tensor_tensor(x_tok[:, NT // 2:NT, :], x_tok[:, NT // 2:NT, :], y[:, NT // 2:NT, :], ALU.add
                                      ).then_inc(mid_high, 1)
                if s == 4:
                    dve.wait_ge(colsum, b * 2 + 1)
                    link(dve.tensor_reduce(gmean[:], stat[:].rearrange("p (g c) -> p g c", c=GROUP), AX.X, ALU.add))
                    for t in range(NT):
                        dve.tensor_tensor(y[:, t, :].rearrange("p (g c) -> p g c", c=GROUP),
                                          x_tok[:, t, :].rearrange("p (g c) -> p g c", c=GROUP),
                                          per_group(gmean[:]), ALU.subtract).then_inc(centred, 1)
                if s == 6:
                    dve.wait_ge(colsum, b * 2 + 2)
                    link(dve.tensor_reduce(gvar[:], stat[:].rearrange("p (g c) -> p g c", c=GROUP), AX.X, ALU.add))
                    dve.tensor_scalar(gvar[:], gvar[:], GN_IN_EPS, None, ALU.add).then_inc(std_in, 1)
                    dve.wait_ge(std_out, b * 3 + 2)
                    dve.reciprocal(grstd[:], gstd[:]).then_inc(grstd_done, 1)
                    dve.wait_ge(grstd_done, b + 1)
                    for t in range(0, NT, 2):
                        tile = y[:, t, :].rearrange("p (g c) -> p g c", c=GROUP)
                        dve.tensor_tensor(tile, tile, per_group(grstd[:]), ALU.mult).then_inc(feat_even, 1)
                if s == 7:
                    dve.wait_ge(std_out, b * 3 + 3)
                    link(dve.tensor_scalar(nstd[:], nstd[:], 1e-12, None, ALU.max))
                    link(dve.reciprocal(nrec[:], nstd[:]))
                    for t in range(NT):
                        dve.tensor_scalar(work[:, t, :], y[:, t, :], nrec[:, t:t + 1], None, ALU.mult
                                          ).then_inc(unit, 1)

            def turn(b, inside):
                if inside:
                    first_best(b - 1, NT - 1)
                for g in range(2 * KC):
                    cols = slice(g % 2 * HALF, (g % 2 + 1) * HALF)
                    dve.wait_ge(high_done, b * 4 * KC + 2 * g + 2)
                    dve.tensor_tensor(n_l[:, g // 2, cols], turned[:, g % BANKS, :],
                                      n_h[:, g // 2, cols].bitcast(F32), ALU.subtract)
                    dve.scalar_tensor_tensor(m_l[:, g // 2, cols], turned[:, g % BANKS, :],
                                             diag[:, g // 2:g // 2 + 1],
                                             m_h[:, g // 2, cols].bitcast(F32), ALU.mult,
                                             ALU.subtract).then_inc(low_done, 1)

            def first_best(b, u):
                dve.wait_ge(rank_done, b * NT + u + 1)
                dve.tensor_reduce(best[:, u % 2, :], ranked[:, u % 2, :].rearrange("p (t m) -> p t m", m=M),
                                  AX.X, ALU.max).then_inc(best_done, 1)
                dve.wait_ge(best_done, b * NT + u + 1)
                if u >= 2:
                    dve.wait_ge(hot_turned, b * NT + u - 1)
                dve.tensor_tensor(onehot[:, u % 2, :].rearrange("p (t m) -> p t m", m=M),
                                  ranked[:, u % 2, :].rearrange("p (t m) -> p t m", m=M),
                                  best[:, u % 2, :].unsqueeze(2).to_broadcast([P, T, M]),
                                  ALU.is_equal).then_inc(hot_done, 1)

            def similar(b, t):
                sims = prod[:, t % 2].rearrange("p h (t m) -> p (h t) m", m=M)
                dve.wait_ge(sim_full, b * NT + t + 1)
                dve.tensor_reduce(top[:, t % 2, :], sims, AX.X, ALU.max).then_inc(best_top, 1)
                if t >= 2:
                    dve.wait_ge(rank_done, b * NT + t - 1)
                dve.wait_ge(best_top, b * NT + t + 1)
                dve.tensor_tensor(equal[:, t % 2, :].rearrange("p (t m) -> p t m", m=M), sims,
                                  top[:, t % 2, :].unsqueeze(2).to_broadcast([P, T, M]),
                                  ALU.is_equal).then_inc(eq_done, 1)
                if t > 0:
                    first_best(b, t - 1)

            pipeline(dve, similar, stage, turn)
            first_best(B - 1, NT - 1)

        @block.tensor
        def _(pe):
            def turn_hot(b, u):
                pe.wait_ge(hot_done, b * NT + u + 1)
                pe.wait_ge(hot_out, b * NT + u + 1)
                for j in range(NT):
                    ins = pe.transpose(oh_ps[:, j, :], onehot[:, u % 2, j * P:(j + 1) * P], ident_b[:])
                ins.then_inc(hot_turned, 1)

            pe.wait_ge(consts, 6)
            pe.wait_ge(w_low, KC)

            def similarities(b, t):
                if t >= 2:
                    pe.wait_ge(eq_done, b * NT + t - 1)
                for h in range(2):
                    for n, (m, u) in enumerate(((m_h, n_h), (m_h, n_l), (m_l, n_h))):
                        for k in range(KC):
                            ins = pe.matmul(prod[:, t % 2, h, :], m[:, k, t * P:(t + 1) * P],
                                            u[:, k, h * HALF:(h + 1) * HALF],
                                            start=n == 0 and k == 0, stop=n == 2 and k == KC - 1)
                ins.then_inc(sim_full, 1)

            def similar(b, t):
                if t == 0:
                    pe.wait_ge(low_done, b * 2 * KC + 2 * KC)
                    similarities(b, 0)
                if t < NT - 1:
                    similarities(b, t + 1)

            def project(b, tiles):
                for t in tiles:
                    if t == 0:
                        pe.wait_ge(o_low, b * KC + KC)
                    if t >= 2:
                        pe.wait_ge(y_done, b * NT + t - 1)
                    for n, (o, w) in enumerate(((o_h, w_h), (o_h, w_l), (o_l, w_h))):
                        for k in range(KC):
                            ins = pe.matmul(proj[:, t % 2, :], o[:, k, t * P:(t + 1) * P], w[:, k, :],
                                            start=n == 0 and k == 0, stop=n == 2 and k == KC - 1)
                    ins.then_inc(prod_full, 1)

            def stage(s, b):
                if s < 2:
                    project(b, (range(2, 5), range(5, NT))[s])
                if s == 2:
                    pe.wait_ge(totals, b * 2 + 1)
                    pe.matmul(stat[:, 0:1], all_avg[:], total, start=True, stop=True).then_inc(averaged, 1)
                if s == 3:
                    pe.wait_ge(totals, b * 2 + 2)
                    pe.matmul(stat[:, 1:2], all_avg[:], sq_c, start=True, stop=True).then_inc(averaged, 1)
                if s == 4:
                    pe.wait_ge(mid_low, b + 1)
                    pe.wait_ge(mid_high, b + 1)
                    for t in range(NT):
                        ins = pe.matmul(stat[:], grp_avg[:], x_tok[:, t, :], start=t == 0, stop=t == NT - 1)
                    ins.then_inc(colsum, 1)
                if s == 5:
                    for t in range(NT):
                        pe.wait_ge(dev_sq, b * NT + t + 1)
                        ins = pe.matmul(stat[:], grp_avg[:], work[:, t, :], start=t == 0, stop=t == NT - 1)
                    ins.then_inc(colsum, 1)

            def turn(b, inside):
                if inside:
                    turn_hot(b - 1, NT - 1)
                if inside:
                    pe.wait_ge(eq_done, b * NT)
                for g in range(2 * KC):
                    pe.wait_ge(unit, b * NT + NT)
                    if g >= BANKS:
                        pe.wait_ge(low_done, b * 2 * KC + g - BANKS + 1)
                    for j in range(4):
                        t = g % 2 * 4 + j
                        ins = pe.transpose(turned[:, g % BANKS, j * P:(j + 1) * P],
                                           work[:, t, g // 2 * P:(g // 2 + 1) * P], ident[:])
                    ins.then_inc(turn_full, 1)
                    if g in (BANKS - 1, BANKS + 1):
                        project(b + 1, [(g - BANKS + 1) // 2])

            project(0, range(2))
            pipeline(pe, similar, stage, turn, turn_hot)
            turn_hot(B - 1, NT - 1)


def convolution_phase(nc, chosen, feat_rows, x_mid, conv_w, conv_b, gamma, beta, out):
    LEAK = 0.01
    TINY = 2.0 ** -60
    ROWS = (P, (KS - P // M) * M)
    STEPS = B * TO
    SETUP = 29
    BANKS = 4
    with ExitStack() as ctx:
        def sb(name, shape, dt=F32):
            return ctx.enter_context(nc.sbuf_tensor("p4_" + name, shape, dt))

        def psum(name, shape, dt=F32):
            return ctx.enter_context(nc.psum_tensor("p4_" + name, shape, dt))

        def sem(name):
            return ctx.enter_context(nc.semaphore("p4_" + name))

        ident = sb("ident", [P, P])
        pick = sb("pick", [8, 2, P])
        w_raw = sb("w_raw", [P, KC, KS])
        w_t = sb("w_t", [8, C])
        taps = sb("taps", [P, 2, C])
        b_row = sb("b_row", [P, C])
        b_col = sb("b_col", [P, 2])
        gam = sb("gam", [P, C])
        bet = sb("bet", [P, C])
        size = sb("size", [P, C])
        sign = sb("sign", [P, C])
        shift = sb("shift", [P, C])
        c_lin = sb("c_lin", [P, C])
        c_abs = sb("c_abs", [P, C])
        win = sb("win", [P, 2, 2, N], F32R)
        blocks = sb("blocks", [P, P // M])
        spot = sb("spot", [P, M])
        high_spot = sb("high_spot", [P, BANKS])
        low_spot = sb("low_spot", [P, BANKS])
        shift_h = sb("shift_h", [P, C], F32R)
        shift_l = sb("shift_l", [P, C], F32R)
        shift_rows = sb("shift_rows", [P, BANKS, C], F32R)
        parts = sb("parts", [P, 2, M], F32R)
        parts_t = sb("parts_t", [P, 2, M])
        level = sb("level", [P, 2, P], F32R)
        f_win = sb("f_win", [P, 2, 2, C])
        tapped = sb("tapped", [P, 2, 2, C])
        tap_sum = sb("tap_sum", [P, 2, 2])
        tap_mean = sb("tap_mean", [P, 2, 2])
        g_h = sb("g_h", [P, 2, 2, C], F32R)
        g_l = sb("g_l", [P, 2, 2, C], F32R)
        junk = sb("junk", [P, BANKS, C])
        sq = sb("sq", [P, 2, BANKS])
        eps = sb("eps", [P, 1])
        std = sb("std", [P, 2, BANKS])
        rstd = sb("rstd", [P, 2, BANKS])
        size_d = sb("size_d", [P, 2, BANKS, C])
        sum_d = sb("sum_d", [P, NT, C])
        sum_abs = sb("sum_abs", [P, NT, C])
        part_d = sb("part_d", [P, NT, C])
        part_abs = sb("part_abs", [P, NT, C])
        mid = sb("mid", [P, NT, C])
        bank = psum("bank", [P, 2, BANKS, C])

        consts = sem("consts")
        c_loaded = sem("c_loaded")
        setup = sem("setup")
        ones_done = sem("ones_done")
        w_turned = sem("w_turned")
        taps_full = sem("taps_full")
        bias_high = sem("bias_high")
        win_loaded = [sem("win_loaded0"), sem("win_loaded1")]
        f_loaded = [sem("f_loaded0"), sem("f_loaded1")]
        tap_done = sem("tap_done")
        mean_done = sem("mean_done")
        high_act = sem("high_act")
        high_pool = sem("high_pool")
        low_done = sem("low_done")
        conv_full = sem("conv_full")
        squared = sem("squared")
        std_done = sem("std_done")
        parts_done = sem("parts_done")
        level_done = sem("level_done")
        shifted = sem("shifted")
        abs_done = sem("abs_done")
        lin_added = sem("lin_added")
        abs_added = sem("abs_added")
        mid_loaded = sem("mid_loaded")
        abs_scaled = sem("abs_scaled")
        lin_scaled = sem("lin_scaled")
        abs_in_mid = sem("abs_in_mid")
        finished = sem("finished")
        stored = sem("stored")
        block = ctx.enter_context(nc.Block())

        def batches(engine, step, scale):
            def batch(b, begins):
                for f in range(2):
                    for g in range(2):
                        if g == 1:
                            step(b, f, f, g, (b, f, 0))
                        elif f == 1:
                            step(b, f, f, g, (b, 0, 1))
                        elif begins:
                            step(b, f, f, g, None)
                        else:
                            step(b, f, f, g, (b - 1, TO - 1, 1))
                            scale(b - 1, 1)
                with engine.Fori(1, TO // 2) as pair:
                    for k in range(2):
                        f = pair * 2 + k
                        for g in range(2):
                            step(b, f, k, g, (b, f, 0) if g == 1 else (b, f - 1, 1))
                scale(b, 0)

            batch(0, True)
            with engine.Fori(1, B) as b:
                batch(b, False)

        @block.sync
        def _(sp):
            with nc.allow_non_contiguous_dma("taps of a channel, once"):
                sp.dma_start(w_raw[:], conv_w.rearrange("(k p) o t -> p k (o t)", p=P)).then_inc(c_loaded, 16)
            sp.dma_start(b_row[96:97, :], conv_b.unsqueeze(0)).then_inc(c_loaded, 16)
            for row, src in ((gam, gamma), (bet, beta)):
                sp.dma_start(row[:], src.partition_broadcast(P)).then_inc(c_loaded, 16)

            def load_features(row, k):
                for c in range(2):
                    sp.dma_start(f_win[0:ROWS[c], k, c, :], feat_rows[bass.ds(row + c * P, ROWS[c]), :]
                                 ).then_inc(f_loaded[k], 16)

            def frame(b, f, k, ahead):
                v = b * TO + f
                sp.wait_ge(tap_done, 2 * v + 2)
                load_features(ahead, k)
                sp.wait_ge(conv_full, NT * v + NT)
                for c in range(2):
                    sp.dma_start(win[0:ROWS[c], k, c, :].bitcast(F32),
                                 chosen[bass.ds(b * N + f * M + c * P, ROWS[c]), :]).then_inc(win_loaded[k], 16)

            def batch(b, first, last):
                for f in range(4):
                    frame(b, f, f % 2, b * N + (2 + f) * M)
                if not first:
                    sp.wait_ge(finished, 2 * b)
                    sp.dma_start(out[bass.ds(b * N - N, N), :].rearrange("(t p) c -> p t c", p=P), mid[:]
                                 ).then_inc(stored, 16)
                with sp.Fori(2, TO // 2 - 1) as pair:
                    for k in range(2):
                        frame(b, pair * 2 + k, k, b * N + (pair * 2 + k + 2) * M)
                if not first:
                    sp.wait_ge(stored, b * 16)
                sp.dma_start(mid[:], x_mid[bass.ds(b * N, N), :].rearrange("(t p) c -> p t c", p=P)
                             ).then_inc(mid_loaded, 16)
                for k in range(2):
                    frame(b, TO - 2 + k, k, k * M if last else b * N + N + k * M)

            for k in range(2):
                load_features(k * M, k)
            batch(0, True, False)
            with sp.Fori(1, B - 1) as b:
                batch(b, False, False)
            batch(B - 1, False, True)
            sp.wait_ge(finished, 2 * B)
            sp.dma_start(out[B * N - N:B * N, :].rearrange("(t p) c -> p t c", p=P), mid[:]).then_inc(stored, 16)
            sp.wait_ge(stored, B * 16)

        @block.gpsimd
        def _(pool):
            pool.memset(ident[:], 0.0).then_inc(consts, 1)
            pool.wait_ge(consts, 1)
            pool.memset(pick[:], 0.0).then_inc(consts, 1)
            pool.wait_ge(consts, 2)
            pool.affine_select(out=ident[:], in_=ident[:], compare_op=ALU.not_equal, fill=1.0, base=0,
                               pattern=[[-1, P]], channel_multiplier=1).then_inc(consts, 1)
            pool.wait_ge(consts, 3)
            spots = pick[:].rearrange("k c (f m) -> k c f m", m=M)
            pool.affine_select(out=spots, in_=spots, compare_op=ALU.not_equal, fill=1.0, base=0,
                               pattern=[[-P // M, 2], [-1, P // M], [0, M]], channel_multiplier=1).then_inc(consts, 1)

            def add(b, v, g):
                pool.wait_ge(abs_done, BANKS * (2 * v + g + 1))
                cols = slice(g * BANKS, (g + 1) * BANKS)
                pool.tensor_tensor(sum_abs[:, cols, :], sum_abs[:, cols, :], size_d[:, g], ALU.add
                                   ).then_inc(abs_added, 1)

            def high(w, k):
                pool.wait_ge(mean_done, w + 1)
                pool.tensor_tensor(g_h[:, k, 0, :], tapped[:, k, 0, :], tap_mean[:, k, 0:1].to_broadcast([P, C]),
                                   ALU.add).then_inc(high_pool, 1)

            def step(b, f, k, g, before):
                if g == 0:
                    high(b * TO + f + 1, 1 - k)
                if before and not (isinstance(before[1], int) and before[1] == 0):
                    bb, ff, gg = before
                    add(bb, bb * TO + ff, gg)

            def scale(b, g):
                pool.wait_ge(abs_added, 1 + (b + 1) * 2 * (TO - 1) - 1 + g)
                cols = slice(g * BANKS, (g + 1) * BANKS)
                pool.tensor_tensor(part_abs[:, cols, :], sum_abs[:, cols, :],
                                   c_abs[:].unsqueeze(1).to_broadcast([P, BANKS, C]), ALU.mult
                                   ).then_inc(abs_scaled, 1)
                pool.wait_ge(mid_loaded, b * 16 + 16)
                pool.wait_ge(abs_scaled, 2 * b + g + 1)
                pool.tensor_tensor(mid[:, cols, :], mid[:, cols, :], part_abs[:, cols, :], ALU.add
                                   ).then_inc(abs_in_mid, 1)

            pool.sem_inc(abs_added, 1)
            high(0, 0)
            pool.wait_ge(setup, SETUP)
            batches(pool, step, scale)
            add(B - 1, STEPS - 1, 1)
            scale(B - 1, 1)

        @block.scalar
        def _(act):
            def square(q, g, j):
                act.wait_ge(conv_full, 2 * NT + BANKS * q + j + 1)
                act.activation(junk[:, j, :], bank[:, g, j, :], ACT.Square,
                               accum_out=sq[:, g, j:j + 1]).then_inc(squared, 1)

            def absolute(b, f, g, j, begins, reused):
                q = 2 * (b * TO + f) + g
                if begins:
                    if not isinstance(b, int):
                        act.wait_ge(abs_scaled, 2 * b - 1 + g)
                    to = sum_abs[:, g * BANKS + j, :]
                else:
                    if reused:
                        act.wait_ge(abs_added, 1 + b * 2 * (TO - 1) + f * 2 - 3 + g)
                    to = size_d[:, g, j, :]
                act.wait_ge(shifted, BANKS * q + j + 1)
                act.activation(to, bank[:, g, j, :], ACT.Abs, scale=rstd[:, g, j:j + 1]).then_inc(abs_done, 1)

            def high(w, k):
                rows = slice(0, ROWS[1])
                act.wait_ge(mean_done, w + 1)
                act.activation(g_h[rows, k, 1, :], tapped[rows, k, 1, :], ACT.Identity,
                               bias=tap_mean[rows, k, 1:2]).then_inc(high_act, 1)

            def step(b, f, k, g, before):
                q = 2 * (b * TO + f) + g

                def last(j):
                    if before:
                        bb, ff, gg = before
                        frame_no = ff if isinstance(ff, int) else None
                        absolute(bb, ff, gg, j, frame_no == 0, frame_no not in (0, 1))

                square(q, g, 0)
                square(q, g, 1)
                last(0)
                square(q, g, 2)
                last(1)
                square(q, g, 3)
                last(2)
                act.wait_ge(squared, BANKS * (q + 1))
                act.activation(std[:, g, :], sq[:, g, :], ACT.Sqrt, scale=1.0 / C, bias=eps[:]).then_inc(std_done, 1)
                three = parts[:, g, 0:3 * BANKS].rearrange("p (j r) -> p j r", r=3)
                act.activation(three[:, :, 0:2], sq[:, g, :].unsqueeze(2).to_broadcast([P, BANKS, 2]), ACT.Sqrt,
                               scale=1.0 / C, bias=eps[:]).then_inc(std_done, 1)
                last(3)
                if g == 0:
                    high(b * TO + f + 1, 1 - k)

            act.wait_ge(ones_done, 4)
            act.wait_ge(setup, 2)
            for k in range(2):
                act.activation(g_h[96:97, k, 1, :], b_row[96:97, :], ACT.Identity, bias=b_col[96:97, 1:2]
                               ).then_inc(bias_high, 1)
            high(0, 0)
            batches(act, step, lambda b, g: None)
            for j in range(BANKS):
                absolute(B - 1, TO - 1, 1, j, False, True)

        @block.vector
        def _(dve):
            done = Chain(dve, setup, 0)
            dve.memset(win[96:97, :, 1, :].bitcast(F32), 1.0).then_inc(ones_done, 1)
            dve.memset(tap_sum[:], 0.0).then_inc(ones_done, 1)
            dve.memset(eps[:], LN_EPS).then_inc(ones_done, 1)
            dve.memset(parts[:].bitcast(F32), 0.0).then_inc(ones_done, 1)
            dve.wait_ge(c_loaded, 64)
            done(dve.tensor_reduce(b_col[96:97, 0:1], b_row[96:97, :], AX.X, ALU.add))
            done(dve.tensor_scalar(b_col[96:97, 1:2], b_col[96:97, 0:1], -1.0 / C, None, ALU.mult))
            dve.wait_ge(bias_high, 2)
            for k in range(2):
                done(dve.scalar_tensor_tensor(g_l[96:97, k, 1, :], b_row[96:97, :], b_col[96:97, 1:2],
                                              g_h[96:97, k, 1, :].bitcast(F32), ALU.add, ALU.subtract))
            dve.wait_ge(w_turned, 1)
            done(dve.tensor_copy(w_t[0:KS, :], bank[0:KS, 0, 0, :]))
            dve.wait_ge(taps_full, 1)
            done(dve.tensor_copy(taps[:], bank[:, 0, 1:3, :]))

            def tap(w, k):
                dve.wait_ge(f_loaded[k], (w - k) * 16 + 32)
                for c in range(2):
                    rows = slice(0, ROWS[c])
                    dve.scalar_tensor_tensor(tapped[rows, k, c, :], f_win[rows, k, c, :], 1.0, taps[rows, c, :],
                                             ALU.mult, ALU.mult,
                                             accum_out=tap_sum[rows, k, c:c + 1]).then_inc(tap_done, 1)
                dve.wait_ge(tap_done, 2 * w + 2)
                dve.tensor_scalar(tap_mean[:, k, :], tap_sum[:, k, :], -1.0 / C, None, ALU.mult
                                  ).then_inc(mean_done, 1)

            def low(w, k):
                for c in range(2):
                    rows = slice(0, ROWS[c])
                    dve.wait_ge((high_pool, high_act)[c], w + 1)
                    ins = dve.scalar_tensor_tensor(g_l[rows, k, c, :], tapped[rows, k, c, :],
                                                   tap_mean[rows, k, c:c + 1], g_h[rows, k, c, :].bitcast(F32),
                                                   ALU.add, ALU.subtract)
                ins.then_inc(low_done, 1)

            def add(v, g, j, begins):
                bank_no = BANKS * (2 * v + g) + j
                dve.wait_ge(abs_done, bank_no + 1)
                total = sum_d[:, g * BANKS + j, :]
                if begins:
                    ins = dve.tensor_scalar(total, bank[:, g, j, :], rstd[:, g, j:j + 1], None, ALU.mult)
                else:
                    dve.wait_ge(lin_added, bank_no + 1)
                    ins = dve.scalar_tensor_tensor(total, bank[:, g, j, :], rstd[:, g, j:j + 1], total,
                                                   ALU.mult, ALU.add)
                ins.then_inc(lin_added, 1)

            def level_rows(q, g):
                dve.wait_ge(std_done, 2 * q + 1)
                dve.reciprocal(rstd[:, g, :], std[:, g, :]).then_inc(parts_done, 1)
                three = parts[:, g, 0:3 * BANKS].rearrange("p (j r) -> p j r", r=3)
                dve.wait_ge(std_done, 2 * q + 2)
                dve.tensor_tensor(three[:, :, 2:3], std[:, g, :].unsqueeze(2), three[:, :, 0:1].bitcast(F32), ALU.subtract
                                  ).then_inc(parts_done, 1)
                dve.wait_ge(parts_done, 3 * q + 2)
                dve.transpose(parts_t[:, g, :], parts[:, g, :].bitcast(F32)).then_inc(parts_done, 1)
                dve.wait_ge(parts_done, 3 * q + 3)
                dve.tensor_tensor(level[:, g, :].rearrange("p (a i) -> p a i", i=M),
                                  parts_t[:, g, :].unsqueeze(1).to_broadcast([P, P // M, M]),
                                  blocks[:].unsqueeze(2).to_broadcast([P, P // M, M]), ALU.mult
                                  ).then_inc(level_done, 1)

            def step(b, f, k, g, before):
                v = b * TO + f
                q = 2 * v + g

                def last(*js):
                    for j in js:
                        if before:
                            bb, ff, gg = before
                            add(bb * TO + ff, gg, j, isinstance(ff, int) and ff == 0)

                last(0, 1)
                last(2)
                level_rows(q, g)
                last(3)
                if g == 0:
                    low(v + 1, 1 - k)
                else:
                    tap(v + 2, k)
                if isinstance(f, int) and f == 1 and not isinstance(b, int):
                    finish(b - 1, g)

            def scale(b, g):
                cols = slice(g * BANKS, (g + 1) * BANKS)
                dve.wait_ge(lin_added, (b + 1) * TO * NT + (g + 1) * BANKS)
                dve.tensor_tensor(part_d[:, cols, :], sum_d[:, cols, :],
                                  c_lin[:].unsqueeze(1).to_broadcast([P, BANKS, C]), ALU.mult
                                  ).then_inc(lin_scaled, 1)

            def finish(b, g):
                cols = slice(g * BANKS, (g + 1) * BANKS)
                dve.wait_ge(lin_scaled, 2 * b + g + 1)
                dve.wait_ge(abs_in_mid, 2 * b + g + 1)
                dve.tensor_tensor(mid[:, cols, :], mid[:, cols, :], part_d[:, cols, :], ALU.add
                                  ).then_inc(finished, 1)

            dve.sem_inc(lin_added, 2 * BANKS)
            tap(0, 0)
            low(0, 0)
            tap(1, 1)
            done(dve.scalar_tensor_tensor(size[:], gam[:], -1.0, gam[:], ALU.mult, ALU.max))
            done(dve.tensor_scalar(size[:], size[:], TINY, None, ALU.max))
            done(dve.tensor_scalar(sign[:], gam[:], 0.0, 2.0, ALU.is_ge, ALU.mult))
            done(dve.tensor_scalar(sign[:], sign[:], -1.0, None, ALU.add))
            done(dve.tensor_tensor(c_lin[:], size[:], sign[:], ALU.mult))
            done(dve.reciprocal(shift[:], c_lin[:]))
            done(dve.tensor_tensor(shift[:], shift[:], bet[:], ALU.mult))
            done(dve.tensor_copy(shift_h[:], shift[:]))
            done(dve.tensor_tensor(shift_l[:], shift[:], shift_h[:].bitcast(F32), ALU.subtract))
            done(dve.tensor_reduce(blocks[:], ident[:].rearrange("p (a i) -> p a i", i=M), AX.X, ALU.add))
            done(dve.tensor_reduce(spot[:], ident[:].rearrange("p (a i) -> p i a", i=M), AX.X, ALU.add))
            three = spot[:, 0:3 * BANKS].rearrange("p (j r) -> p j r", r=3)
            done(dve.tensor_tensor(high_spot[:].unsqueeze(2), three[:, :, 0:1], three[:, :, 2:3], ALU.add))
            done(dve.tensor_copy(low_spot[:].unsqueeze(2), three[:, :, 1:2]))
            for j in range(BANKS):
                done(dve.tensor_scalar(part_d[:, j, :], shift_l[:].bitcast(F32), low_spot[:, j:j + 1], None, ALU.mult))
                done(dve.scalar_tensor_tensor(shift_rows[:, j, :], shift_h[:].bitcast(F32), high_spot[:, j:j + 1],
                                              part_d[:, j, :], ALU.mult, ALU.add))
            done(dve.tensor_scalar(c_lin[:], c_lin[:], 0.5 * (1.0 + LEAK) / TO, None, ALU.mult))
            done(dve.tensor_scalar(c_abs[:], size[:], 0.5 * (1.0 - LEAK) / TO, None, ALU.mult))
            assert done.n == SETUP, done.n
            batches(dve, step, scale)
            for j in range(BANKS):
                add(STEPS - 1, 1, j, False)
            scale(B - 1, 1)
            for g in range(2):
                finish(B - 1, g)

        @block.tensor
        def _(pe):
            pe.sem_inc(conv_full, 2 * NT)
            pe.wait_ge(consts, 4)
            pe.wait_ge(c_loaded, 64)
            for k in range(KC):
                ins = pe.transpose(bank[0:KS, 0, 0, k * P:(k + 1) * P], w_raw[:, k, :], ident[:])
            ins.then_inc(w_turned, 1)
            pe.wait_ge(setup, 5)
            for c in range(2):
                ins = pe.matmul(bank[:, 0, 1 + c, :], pick[0:KS, c, :], w_t[0:KS, :], start=True, stop=True)
            ins.then_inc(taps_full, 1)
            pe.wait_ge(ones_done, 2)

            def fill(v, k, g, j):
                pe.wait_ge(low_done, v + 1)
                pe.wait_ge(win_loaded[k], (v - k) * 16 + 32)
                pe.wait_ge(lin_added, BANKS * (2 * v + g) + j + 1)
                t = g * BANKS + j
                for c in range(2):
                    rows = slice(0, ROWS[c] + c)
                    for part, gg in enumerate((g_h, g_l)):
                        ins = pe.matmul(bank[:, g, j, :], win[rows, k, c, t * P:(t + 1) * P],
                                        gg[rows, k, c, :], start=c == 0 and part == 0,
                                        stop=c == 1 and part == 1)
                ins.then_inc(conv_full, 1)

            def lift(q, g, j):
                pe.wait_ge(level_done, q + 1)
                pe.matmul(bank[:, g, j, :], level[:, g, :], shift_rows[:, j, :], start=False, stop=True,
                          skip_group_check=True
                          ).then_inc(shifted, 1)

            def step(b, f, k, g, before):
                v = b * TO + f

                def last(*js):
                    for j in js:
                        if before:
                            lift(2 * v + g - 1, before[2], j)

                for j in range(3):
                    fill(v, k, g, j)
                last(0, 1)
                fill(v, k, g, 3)
                last(2, 3)

            batches(pe, step, lambda b, g: None)
            for j in range(BANKS):
                lift(2 * STEPS - 1, 1, j)


def diagonal(w):
    n = w.shape[0]
    return w.rearrange("a b -> (a b)")[0:n * n:n + 1].rearrange("(k p) -> p k", p=P)


def build(nc, x, w_qkv, w_out, b_out, gn_gamma, gn_beta, w_mix, conv_w, conv_b, ln_gamma, ln_beta, out):
    def scratch(name, shape):
        return nc.dram_tensor(name, shape, F32, kind="Internal").ap()

    qk_hi = scratch("qk_hi", (2 * B * C, N))
    qk_lo = scratch("qk_lo", (2 * B * C, N))
    v_split = scratch("v_split", (G, P, NT, 2 * D))
    attended = scratch("attended", (G, N, D))
    x_mid = scratch("x_mid", (B * N, C))
    feat_rows = scratch("feat_rows", (B * N, C))
    chosen = scratch("chosen", (B * N, N))
    project_phase(nc, x, w_qkv, qk_hi, qk_lo, v_split)
    attention_phase(nc, qk_hi, qk_lo, v_split, attended)
    mixing_phase(nc, x, attended, w_out, b_out, gn_gamma, gn_beta, diagonal(w_mix), x_mid, feat_rows, chosen)
    convolution_phase(nc, chosen, feat_rows, x_mid, conv_w, conv_b, ln_gamma, ln_beta, out)


_INS = ["x", "L0_conv_w_qkv", "L0_conv_w_out", "L0_conv_b_out", "L0_conv_gamma", "L0_conv_beta", "L1_conv_W",
        "L1_conv_conv_w", "L1_conv_conv_b", "L1_conv_ln_gamma", "L1_conv_ln_beta"]


def kernel(**inputs):
    import numpy as np
    import concourse.bacc as bacc
    from concourse.bass_utils import run_bass_kernel_spmd

    nc = bacc.Bacc("TRN2", target_bir_lowering=False, num_devices=1)
    arrays, args = {}, []
    for name in _INS:
        a = np.ascontiguousarray(inputs[name])
        if name == "x":
            a = a.reshape(B * N, C)
        arrays["in_" + name] = a
        args.append(nc.dram_tensor("in_" + name, a.shape, mybir.dt.from_np(a.dtype), kind="ExternalInput").ap())
    out = nc.dram_tensor("out", (B * N, C), F32, kind="ExternalOutput").ap()
    build(nc, *args, out)
    r = run_bass_kernel_spmd(nc, [arrays], core_ids=[0])
    return r.results[0]["out"].reshape(8, 32, 32, 512)
```
